# Optimizing a Trainium2 kernel written in Bass

```python
import numpy as np
import jax
import jax.numpy as jnp

def _softmax(x, axis=-1):
    return jax.nn.softmax(x, axis=axis)

def _gelu(x):
    return jax.nn.gelu(x, approximate=True)

def _silu(x):
    return jax.nn.silu(x)

def _sigmoid(x):
    return jax.nn.sigmoid(x)

def _layernorm(x, axis=-1, eps=1e-05):
    m = jnp.mean(x, axis=axis, keepdims=True)
    v = jnp.var(x, axis=axis, keepdims=True)
    return (x - m) / jnp.sqrt(v + eps)

def _scatter_add(tgt, idx, src, axis=0):
    return tgt.at[idx].add(src)

def _segment_sum(src, seg, n):
    return jax.ops.segment_sum(src, seg, n)
kernel_name = 'mk_flamingo_gated_d1_seqx_r2_a09311'

def setup_inputs(seed: int=0):
    np.random.seed(seed)
    _w = jnp.asarray

    def _rec_inputs():
        import jax
        import jax.numpy as jnp
        _rk = jax.random.key(seed)
        x = -0.000125 + 0.9999 * jax.random.normal(jax.random.fold_in(_rk, 1), (2, 1024, 2048), jnp.float32)
        _lenS = 1024 - jax.random.randint(jax.random.fold_in(_rk, 7), (2,), 0, max(1, 1024 // 4) + 1, jnp.int32)
        _lenS2 = 2048 - jax.random.randint(jax.random.fold_in(_rk, 8), (2,), 0, max(1, 2048 // 4) + 1, jnp.int32)
        _ctx_4096P = jax.random.normal(jax.random.fold_in(_rk, 11), (2, 16, 2048), jnp.float32)
        _ctx_4096c = jax.random.dirichlet(jax.random.fold_in(_rk, 511), 0.3 * jnp.ones((16,), jnp.float32), (2, 2048))
        _ctx_4096t = jnp.einsum('bsk,bkd->bsd', _ctx_4096c, _ctx_4096P)
        _ctx_4096t = _ctx_4096t * jax.lax.rsqrt(jnp.mean(jnp.square(_ctx_4096t)) + 1e-12) * 0.953939
        ctx_4096 = -5.72187e-05 + 0.999849 * (_ctx_4096t + 0.3 * jax.random.normal(jax.random.fold_in(_rk, 611), (2, 2048, 2048), jnp.float32))
        _g = jax.random.normal(jax.random.fold_in(_rk, 9001), (2, 1), jnp.float32)
        _g = jnp.sign(_g) * jnp.maximum(jnp.abs(_g), 1.0) + (_g == 0) * 1.0
        g_xattn = _g[0]
        g_ffn = _g[1]
        return (x, ctx_4096, g_xattn, g_ffn)
    x, ctx_4096, g_xattn, g_ffn = _rec_inputs()

    def _L0_xattn_setup():
        import jax, jax.numpy as jnp
        import numpy as np
        QMIN = 0.0
        QMAX = 255.0

        def fake_quant(x, scale, zp):
            s = scale.reshape(())
            z = zp.reshape(())
            q = jnp.clip(jnp.round(x / s + z), QMIN, QMAX)
            return (q - z) * s
        key = jax.random.key(seed)
        k1, k2 = jax.random.split(key)
        B, M, K, N = (4, 1024, 2048, 2048)
        x1 = jax.random.normal(k1, (B, M, K), dtype=jnp.float32)
        x2 = jax.random.normal(k2, (B, K, N), dtype=jnp.float32)
        x1_scale = jnp.full((1,), 8.0 / 255.0, dtype=jnp.float32)
        x1_zp = jnp.full((1,), 128.0, dtype=jnp.float32)
        x2_scale = jnp.full((1,), 8.0 / 255.0, dtype=jnp.float32)
        x2_zp = jnp.full((1,), 128.0, dtype=jnp.float32)
        return {'x1': x1, 'x2': x2, 'x1_scale': x1_scale, 'x1_zp': x1_zp, 'x2_scale': x2_scale, 'x2_zp': x2_zp}
    _L0_xattn_all = _L0_xattn_setup()
    _L0_xattn_in = {k: v for k, v in _L0_xattn_all.items() if k in ('x1_scale', 'x1_zp', 'x2_scale', 'x2_zp')}
    del _L0_xattn_all

    def _L0_ffn_setup():
        import jax, jax.numpy as jnp
        import numpy as np
        R = 16
        LORA_ALPHA = 16
        SCALING = LORA_ALPHA / R
        key = jax.random.key(seed)
        kx, kr, ka = jax.random.split(key, 3)
        B, S, D, DO, E = (4, 1024, 2048, 2048, 8)
        x = jax.random.normal(kx, (B, S, D), dtype=jnp.float32)
        bound_r = 1.0 / np.sqrt(D)
        route_w = jax.random.uniform(kr, (E, D), jnp.float32, -bound_r, bound_r)
        bound_a = 1.0 / np.sqrt(D)
        A = jax.random.uniform(ka, (E, R, D), jnp.float32, -bound_a, bound_a)
        kb = jax.random.fold_in(key, 7)
        Bw = jax.random.normal(kb, (E, DO, R), dtype=jnp.float32) * 0.02
        return {'x': x, 'route_w': route_w, 'A': A, 'Bw': Bw}
    _L0_ffn_all = _L0_ffn_setup()
    _L0_ffn_in = {k: v for k, v in _L0_ffn_all.items() if k in ('route_w', 'A', 'Bw')}
    del _L0_ffn_all
    return {'x': x, 'ctx_4096': ctx_4096, 'g_xattn': g_xattn, 'g_ffn': g_ffn, 'L0_xattn_x1_scale': _L0_xattn_in['x1_scale'], 'L0_xattn_x1_zp': _L0_xattn_in['x1_zp'], 'L0_xattn_x2_scale': _L0_xattn_in['x2_scale'], 'L0_xattn_x2_zp': _L0_xattn_in['x2_zp'], 'L0_ffn_route_w': _L0_ffn_in['route_w'], 'L0_ffn_A': _L0_ffn_in['A'], 'L0_ffn_Bw': _L0_ffn_in['Bw']}

def reference(x, ctx_4096, g_xattn, g_ffn, L0_xattn_x1_scale, L0_xattn_x1_zp, L0_xattn_x2_scale, L0_xattn_x2_zp, L0_ffn_route_w, L0_ffn_A, L0_ffn_Bw):
    import jax
    import jax.numpy as jnp

    def _L0_xattn_ref(x1, x2, x1_scale, x1_zp, x2_scale, x2_zp):
        import jax, jax.numpy as jnp
        import numpy as np
        QMIN = 0.0
        QMAX = 255.0

        def fake_quant(x, scale, zp):
            s = scale.reshape(())
            z = zp.reshape(())
            q = jnp.clip(jnp.round(x / s + z), QMIN, QMAX)
            return (q - z) * s
        q1 = fake_quant(x1, x1_scale, x1_zp)
        q2 = fake_quant(x2, x2_scale, x2_zp)
        return jnp.matmul(q1, q2)

    def _L0_ffn_ref(x, route_w, A, Bw):
        import jax, jax.numpy as jnp
        import numpy as np
        R = 16
        LORA_ALPHA = 16
        SCALING = LORA_ALPHA / R
        logits = jnp.einsum('bsd,ed->bse', x, route_w)
        topk_v, topk_idx = jax.lax.top_k(logits, 1)
        E = logits.shape[-1]
        route_weight = jax.nn.one_hot(topk_idx[..., 0], E, dtype=logits.dtype) * topk_v
        h = jnp.einsum('bsd,erd->bser', x, A)
        wh = route_weight[..., None] * h
        out = jnp.einsum('bser,eor->bso', wh, Bw) * SCALING
        return out
    x = x + jnp.tanh(g_xattn[0]) * _L0_xattn_ref(_layernorm(x, axis=-1), ctx_4096, L0_xattn_x1_scale, L0_xattn_x1_zp, L0_xattn_x2_scale, L0_xattn_x2_zp)
    x = x + jnp.tanh(g_ffn[0]) * _L0_ffn_ref(_layernorm(x, axis=-1), L0_ffn_route_w, L0_ffn_A, L0_ffn_Bw)
    return x

_drawn_inputs = setup_inputs


def setup_inputs(seed=0):
    import zlib

    import numpy as np

    out = dict(_drawn_inputs(seed))
    spreads = {}
    factors = {'L0_ffn_route_w': 8.0, 'L0_ffn_A': 8.0, 'L0_ffn_Bw': 8.0}
    for name, (base, spread) in spreads.items():
        noise = np.random.default_rng([zlib.crc32(name.encode()), seed]).standard_normal(out[name].shape)
        drawn = base * np.exp(spread * noise) if base else spread * noise
        out[name] = jnp.asarray(drawn.astype(out[name].dtype))
    for name, factor in factors.items():
        out[name] = (out[name] * factor).astype(out[name].dtype)
    return out
```

```python
from contextlib import ExitStack

import numpy as np
import concourse.bass as bass
from concourse import mybir

P = 128
B, M, D = 2, 1024, 2048
CTX = 2048
E, R = 8, 16
ER = E * R
TB = M // P
T = B * TB
KC = D // P
NW = 512
NB = D // NW
SLOTS = 6
PIECES = 4
PK = KC // PIECES
XS = 4
WC = ER + E
GK = KC // 4
EPS = 1e-5
QMAX = 255.0
ZC = 128.0
ROUND = 12582912.0
YS = 1024.0
WS = 32768.0
TINY = 1e-30


class Count:

    def __init__(self, reg, step, start):
        self.reg, self.step, self.start = reg, step, start

    def __add__(self, n):
        return Count(self.reg, self.step, self.start + n)

    def __sub__(self, n):
        return self + -n

    def __mul__(self, n):
        return Count(self.reg, self.step * n, self.start * n)

    __radd__, __rmul__ = __add__, __mul__

    def value(self):
        return self.reg * self.step + self.start


def at(n):
    return n if isinstance(n, int) else n.value()


def due(n):
    return not isinstance(n, int) or n > 0


def half(n):
    return n // 2 if isinstance(n, int) else Count(n.reg, n.step // 2, n.start // 2)


def build(nc, x, ctx, g_x, g_f, x1_scale, x1_zp, x2_scale, x2_zp, route_w, A, Bw, out):
    f32, bf16, f16 = mybir.dt.float32, mybir.dt.bfloat16, mybir.dt.float16
    i32, u32 = mybir.dt.int32, mybir.dt.uint32
    ALU = mybir.AluOpType
    ACT = mybir.ActivationFunctionType
    AX = mybir.AxisListType

    x_t = x.rearrange("b (t p) n -> (b t) p n", p=P)
    out_t = out.rearrange("b (t p) n -> (b t) p n", p=P)
    ctx_k = ctx.rearrange("b (c p) n -> b p c n", p=P)
    A_v = A.rearrange("e r d -> (e r) d")
    B_v = Bw.rearrange("e (p j) r -> p e j r", p=P)

    st = ExitStack()
    with st:
        def sb(name, shape, dt):
            return st.enter_context(nc.sbuf_tensor(name, shape, dt))

        def bank(name):
            return st.enter_context(nc.psum_tensor(name, [P, NW], f32))

        def sem(name):
            return st.enter_context(nc.semaphore(name))

        s_x_loaded = [sem("x_loaded0"), sem("x_loaded1")]
        s_ctx_loaded = [sem("ctx_loaded0"), sem("ctx_loaded1")]
        s_par_loaded = sem("par_loaded")
        s_a_loaded = sem("a_loaded")
        s_r_loaded = sem("r_loaded")
        s_b_loaded = sem("b_loaded")
        s_stored = sem("stored")
        s_id_zero = sem("id_zero")
        s_idf_made = sem("idf_made")
        s_consts = sem("consts")
        s_mexp_set = sem("mexp_set")
        s_eid_made = sem("eid_made")
        s_eid_ready = sem("eid_ready")
        s_inv_done = sem("inv_done")
        s_par_ready = sem("par_ready")
        s_dz_done = sem("dz_done")
        s_nz_done = sem("nz_done")
        s_flag_ready = sem("flag_ready")
        s_tanh_done = sem("tanh_done")
        s_s12_done = sem("s12_done")
        s_cc_done = sem("cc_done")
        s_cd_done = sem("cd_done")
        s_kdd_done = sem("kdd_done")
        s_wmax_step = sem("wmax_step")
        s_rmax_step = sem("rmax_step")
        s_bmax_step = sem("bmax_step")
        s_a_scaled = sem("a_scaled")
        s_r_scaled = sem("r_scaled")
        s_a_turned = sem("a_turned")
        s_r_turned = sem("r_turned")
        s_a_high = sem("a_high")
        s_r_high = sem("r_high")
        s_a_low = sem("a_low")
        s_r_low = sem("r_low")
        s_b_permuted = sem("b_permuted")
        s_b_turned = sem("b_turned")
        s_b_raw = sem("b_raw")
        s_b_high = sem("b_high")
        s_weights_ready = sem("weights_ready")
        s_wsc_step = sem("wsc_step")
        s_diag_ready = sem("diag_ready")
        s_scales_spread = sem("scales_spread")
        s_wscale_ready = sem("wscale_ready")
        s_ctx_affine = sem("ctx_affine")
        s_ctx_rounded = sem("ctx_rounded")
        s_ctx_ready = sem("ctx_ready")
        s_bn1_done = sem("bn1_done")
        s_stats1 = sem("stats1")
        s_ve1_done = sem("ve1_done")
        s_rs1_done = sem("rs1_done")
        s_na1_done = sem("na1_done")
        s_norm1 = sem("norm1")
        s_affine1 = sem("affine1")
        s_x_rounded = sem("x_rounded")
        s_q1_ready = sem("q1_ready")
        s_q1T_turned = sem("q1T_turned")
        s_q1T_ready = sem("q1T_ready")
        s_main_done = sem("main_done")
        s_main_added = sem("main_added")
        s_bn2_done = sem("bn2_done")
        s_stats2 = sem("stats2")
        s_ve2_done = sem("ve2_done")
        s_rs2_done = sem("rs2_done")
        s_na2_done = sem("na2_done")
        s_norm2 = sem("norm2")
        s_y_ready = sem("y_ready")
        s_y_turned = sem("y_turned")
        s_y_high = sem("y_high")
        s_y_split = sem("y_split")
        s_h_done = sem("h_done")
        s_hs_done = sem("hs_done")
        s_h_read = sem("h_read")
        s_hl_done = sem("hl_done")
        s_top_done = sem("top_done")
        s_idx_done = sem("idx_done")
        s_idxf_done = sem("idxf_done")
        s_pick_done = sem("pick_done")
        s_wh_done = sem("wh_done")
        s_am_done = sem("am_done")
        s_floor_done = sem("floor_done")
        s_rec_done = sem("rec_done")
        s_tsc_done = sem("tsc_done")
        s_fac_done = sem("fac_done")
        s_wh_high = sem("wh_high")
        s_wh_ready = sem("wh_ready")
        s_wh_turned = sem("wh_turned")
        s_whT_ready = sem("whT_ready")
        s_out_done = sem("out_done")
        s_outp_read = sem("outp_read")
        s_colsum_done = sem("colsum_done")
        s_corr_ready = sem("corr_ready")
        s_rowsum_done = sem("rowsum_done")
        s_rowc_ready = sem("rowc_ready")
        s_terms_added = sem("terms_added")
        s_passed = sem("passed")

        q2 = sb("q2", [P, SLOTS, KC, NW], bf16)
        xs = sb("xs", [P, XS, D], f32)
        q1 = sb("q1", [P, D], bf16)
        q1T = sb("q1T", [P, 2, KC, P], bf16)
        xw = sb("xw", [P, D], f32)
        stage = sb("stage", [P, 2, PK * NW], f32)
        y = sb("y", [P, D], f32)
        yhi = sb("yhi", [P, 2, GK * P], f16)
        ylo = sb("ylo", [P, 2, GK * P], f16)
        WT = sb("WT", [P, KC, 2 * WC], f16)
        BT = sb("BT", [P, 2, D], f16)
        hs = sb("hs", [P, WC], f32)
        hl = sb("hl", [P, WC], f32)
        wscale = sb("wscale", [P, WC], f32)
        top8 = sb("top8", [P, 8], f32)
        idx8 = sb("idx8", [P, 8], u32)
        idxf = sb("idxf", [P, 1], f32)
        pick = sb("pick", [P, ER], f32)
        wh = sb("wh", [P, ER], f32)
        whs = sb("whs", [P, 2, ER], f16)
        whT = sb("whT", [P, 2, P], f16)
        am = sb("am", [P, 4], f32)
        tsc = sb("tsc", [P, 2], f32)
        eid_i = wh[:, :].bitcast(i32)
        eid = sb("eid", [P, ER], f32)
        idf = sb("idf", [P, P], f32)
        idb = sb("idb", [P, P], bf16)
        idh = sb("idh", [P, P], f16)
        onesf = sb("onesf", [P, P], f32)
        onesb = sb("onesb", [P, P], bf16)
        diag = pick
        diag8 = sb("diag8", [E, E], f32)
        par = sb("par", [P, 8], f32)
        inv = sb("inv", [P, 2], f32)
        ninv = sb("ninv", [P, 1], f32)
        th = sb("th", [P, 2], f32)
        c12 = sb("c12", [P, 2], f32)
        cc = sb("cc", [P, 1], f32)
        dz = sb("dz", [P, 2], f32)
        cd = sb("cd", [P, 2], f32)
        kdd = sb("kdd", [P, 2], f32)
        nz = sb("nz", [P, 2], f32)
        flag = sb("flag", [P, 1], f32)
        mexp = sb("mexp", [P, 1], f32)
        bn1 = sb("bn1", [P, NB, 6], f32)
        bn2 = sb("bn2", [P, NB, 6], f32)
        mv1 = sb("mv1", [P, 2, 2], f32)
        mv2 = sb("mv2", [P, 2, 2], f32)
        ve1 = sb("ve1", [P, 2], f32)
        ve2 = sb("ve2", [P, 2], f32)
        rs1 = sb("rs1", [P, 2], f32)
        rs2 = sb("rs2", [P, 2], f32)
        sc1 = sb("sc1", [P, 2, 3], f32)
        sc2 = sb("sc2", [P, 2, 3], f32)
        rowc = sb("rowc", [P, 2, 2], f32)
        corr = sb("corr", [P, D], f32)
        wmax = sb("wmax", [P, 4], f32)
        rmax = sb("rmax", [E, 4], f32)
        bmax = sb("bmax", [P, 4], f32)
        wsc = sb("wsc", [P, 2], f32)
        rsc = sb("rsc", [E, 1], f32)

        mainp = [bank("main0"), bank("main1")]
        turn = [bank("turn0"), bank("turn1")]
        turnb = [t[:, :].bitcast(bf16) for t in turn]
        hp = bank("hp")
        wp = bank("wp")
        wph = wp[:, :].bitcast(f16)
        outp = [bank("outp0"), bank("outp1")]

        scr = [q2[:, s, :, :].rearrange("p k n -> p (k n)").bitcast(f32) for s in (SLOTS - 2, SLOTS - 1)]
        a_nat, r_nat = scr[0][:, 0:D], scr[0][0:E, D:2 * D]
        b_nat, b_perm = scr[1][:, 0:D], scr[1][:, D:2 * D]
        b_raw = b_nat

        def xcol(t, c0, c1):
            if isinstance(t, int):
                return xs[:, t % XS, c0:c1]
            return xs[:, bass.ds(at(t) % XS, 1), c0:c1].rearrange("p a n -> p (a n)")

        def slot(block):
            return block % SLOTS

        def stage_of(piece):
            return piece % 2

        def schedule(eng, f, drain=0):
            f(0, 0)
            f(1, 1)
            with eng.Fori(0, TB // 2 - 1) as pair:
                t = Count(pair, 2, 2)
                f(t, 0)
                f(t + 1, 1)
            f(TB, 0)
            f(TB + 1, 1)
            with eng.Fori(0, (T - TB) // 2 - 2) as pair:
                t = Count(pair, 2, TB + 2)
                f(t, 0)
                f(t + 1, 1)
            for t in range(T - 2, T + drain):
                f(t, t % 2)

        def has(t, d):
            return not isinstance(t, int) or 0 <= t + d < T

        EARLY = NB * PIECES
        block_ = st.enter_context(nc.Block())

        @block_.sync
        def _(sp):
            def load_x(t, pt):
                src = x_t[t] if isinstance(t, int) else x_t[bass.ds(at(t), 1)].rearrange("a p n -> p (a n)")
                sp.dma_start(xcol(t, 0, D), src).then_inc(s_x_loaded[pt], 16)

            def load_ctx(piece, n=None):
                b, nb, q = piece // (NB * PIECES), piece // PIECES % NB, piece % PIECES
                if due(piece - 1):
                    sp.wait_ge(s_ctx_ready, at(piece - 1))
                sp.dma_start(stage[:, stage_of(piece), :].rearrange("p (c n) -> p c n", c=PK),
                             ctx_k[b, :, q * PK:(q + 1) * PK, nb * NW:(nb + 1) * NW])\
                  .then_inc(s_ctx_loaded[piece % 2], 16)

            for n, v in enumerate((x1_scale, x2_scale, x1_zp, x2_zp, g_x, g_f)):
                sp.dma_start(par[:, n:n + 1], v.partition_broadcast(P)).then_inc(s_par_loaded, 16)
            load_x(0, 0)
            load_ctx(0)
            load_ctx(1)
            sp.dma_start(a_nat, A_v).then_inc(s_a_loaded, 16)
            sp.dma_start(r_nat, route_w).then_inc(s_r_loaded, 16)
            sp.dma_start(b_nat.rearrange("p (e j r) -> p e (j r)", e=E, r=R),
                         B_v.rearrange("p e j r -> p e (j r)")).then_inc(s_b_loaded, 16)
            for piece in range(2, EARLY):
                load_ctx(piece)
                if piece == 2 * PIECES:
                    load_x(1, 1)

            def period(t, pt):
                if isinstance(t, int):
                    if t == 0:
                        load_ctx(EARLY)
                    if t < TB - 1:
                        load_ctx(EARLY + t + 1)
                    if t == TB:
                        for piece in range(EARLY + TB, 2 * EARLY):
                            load_ctx(piece)
                else:
                    loop_ctx(t, pt)
                if has(t, -2):
                    sp.wait_ge(s_outp_read, at(2 + NB * (t - 1)))
                    dst = out_t[t - 2] if isinstance(t, int) else out_t[bass.ds(at(t - 2), 1)].rearrange("a p n -> p (a n)")
                    sp.dma_start(dst, xcol(t - 2, 0, D)).then_inc(s_stored, 16)
                if has(t, 2) and (not isinstance(t, int) or t >= 0):
                    if due(16 * (t - 1)):
                        sp.wait_ge(s_stored, at(16 * (t - 1)))
                    load_x(t + 2, pt)

            in_batch0 = [True]

            def loop_ctx(t, pt):
                if not in_batch0[0]:
                    return
                n = t + 1
                sp.wait_ge(s_ctx_ready, at(EARLY + n - 1))
                src = ctx_k[1, :, bass.ds(at(n) % PIECES * PK, PK), bass.ds(at(n) // PIECES * NW, NW)]
                sp.dma_start(stage[:, (pt + 1) % 2, :].rearrange("p (c n) -> p c n", c=PK), src)\
                  .then_inc(s_ctx_loaded[1 - pt], 16)

            period(0, 0)
            period(1, 1)
            with sp.Fori(0, TB // 2 - 2) as pair:
                t = Count(pair, 2, 2)
                period(t, 0)
                period(t + 1, 1)
            period(TB - 2, 0)
            period(TB - 1, 1)
            period(TB, 0)
            period(TB + 1, 1)
            in_batch0[0] = False
            with sp.Fori(0, (T - TB) // 2 - 2) as pair:
                t = Count(pair, 2, TB + 2)
                period(t, 0)
                period(t + 1, 1)
            for t in range(T - 2, T + 2):
                period(t, t % 2)
            sp.wait_ge(s_stored, at(16 * T))

        @block_.gpsimd
        def _(pool):
            pool.memset(idf[:, :], 0.0).then_inc(s_id_zero, 1)
            pool.sem_inc(s_outp_read, 2)
            pool.memset(onesf[:, :], 1.0).then_inc(s_consts, 1)
            pool.memset(onesb[:, :], 1.0).then_inc(s_consts, 1)
            pool.memset(mexp[:, :], -0.5).then_inc(s_mexp_set, 1)
            pool.iota(eid_i, pattern=[[1, E], [0, R]], base=0, channel_multiplier=0).then_inc(s_eid_made, 1)
            pool.wait_ge(s_id_zero, 1)
            pool.affine_select(out=idf[:, :], in_=idf[:, :], compare_op=ALU.not_equal, fill=1.0, base=0,
                               pattern=[[-1, P]], channel_multiplier=1).then_inc(s_idf_made, 1)
            pool.wait_ge(s_idf_made, 1)
            pool.tensor_copy(idb[:, :], idf[:, :]).then_inc(s_consts, 1)
            pool.tensor_copy(idh[:, :], idf[:, :]).then_inc(s_consts, 1)
            pool.wait_ge(s_eid_made, 1)
            pool.tensor_copy(eid[:, :], eid_i).then_inc(s_eid_ready, 1)

            def first_norm(t, pt):
                pool.wait_ge(s_stats1, at(t + 1))
                pool.sem_inc(s_passed, 1)
                if isinstance(t, int) and t == 0:
                    pool.wait_ge(s_par_ready, 1)
                    pool.wait_ge(s_mexp_set, 1)
                if due(t - 1):
                    pool.wait_ge(s_affine1, at(t - 1))
                pool.sem_inc(s_passed, 1)
                pool.tensor_scalar(ve1[:, pt:pt + 1], mv1[:, pt, 1:2], EPS, None, ALU.add).then_inc(s_ve1_done, 1)
                pool.wait_ge(s_ve1_done, at(t + 1))
                pool.tensor_tensor(rs1[:, pt:pt + 1], ve1[:, pt:pt + 1], mexp[:, :], ALU.pow).then_inc(s_rs1_done, 1)
                pool.wait_ge(s_rs1_done, at(t + 1))
                pool.tensor_tensor(sc1[:, pt, 0:1], rs1[:, pt:pt + 1], ninv[:, :], ALU.mult).then_inc(s_na1_done, 1)
                pool.tensor_tensor(sc1[:, pt, 1:2], rs1[:, pt:pt + 1], inv[:, 0:1], ALU.mult)
                pool.wait_ge(s_na1_done, at(t + 1))
                pool.sem_inc(s_passed, 1)
                pool.tensor_scalar(sc1[:, pt, 2:3], mv1[:, pt, 0:1], sc1[:, pt, 0:1], par[:, 2:3], ALU.mult, ALU.add)\
                    .then_inc(s_norm1, 1)

            def second_norm(t, pt):
                pool.wait_ge(s_stats2, at(t + 1))
                if due(t - 1):
                    pool.wait_ge(s_y_ready, at(t - 1))
                pool.sem_inc(s_passed, 1)
                pool.tensor_scalar(ve2[:, pt:pt + 1], mv2[:, pt, 1:2], EPS, None, ALU.add).then_inc(s_ve2_done, 1)
                pool.wait_ge(s_ve2_done, at(t + 1))
                pool.tensor_tensor(rs2[:, pt:pt + 1], ve2[:, pt:pt + 1], mexp[:, :], ALU.pow).then_inc(s_rs2_done, 1)
                pool.wait_ge(s_rs2_done, at(t + 1))
                pool.sem_inc(s_passed, 1)
                pool.tensor_scalar(sc2[:, pt, 0:1], rs2[:, pt:pt + 1], -YS, None, ALU.mult).then_inc(s_na2_done, 1)
                pool.tensor_scalar(sc2[:, pt, 1:2], rs2[:, pt:pt + 1], YS, None, ALU.mult)
                pool.wait_ge(s_na2_done, at(t + 1))
                pool.tensor_tensor(sc2[:, pt, 2:3], mv2[:, pt, 0:1], sc2[:, pt, 0:1], ALU.mult).then_inc(s_norm2, 1)

            first_norm(0, 0)
            pool.wait_ge(s_b_loaded, 16)
            pool.tensor_copy(b_perm.rearrange("p (j e r) -> p e j r", e=E, r=R),
                             b_nat.rearrange("p (e j r) -> p e j r", e=E, r=R)).then_inc(s_b_permuted, 1)

            def period(t, pt):
                if has(t, 1):
                    first_norm(t + 1, 1 - pt)
                second_norm(t, pt)

            schedule(pool, period)

        @block_.scalar
        def _(act):
            act.wait_ge(s_par_loaded, 16 * 6)
            act.activation(th[:, :], par[:, 4:6], ACT.Tanh).then_inc(s_tanh_done, 1)

            def affine_ctx(piece, n=None):
                s = stage_of(piece) if n is None else n
                act.wait_ge(s_ctx_loaded[s], at(16 * (half(piece) + 1)))
                act.activation(stage[:, s, :], stage[:, s, :], ACT.Relu, bias=par[:, 3:4], scale=inv[:, 1:2])\
                   .then_inc(s_ctx_affine, 1)

            def affine_x(t, pt):
                act.wait_ge(s_norm1, at(t + 1))
                if due(t):
                    act.wait_ge(s_q1_ready, at(t))
                act.activation(xw[:, :], xcol(t, 0, D), ACT.Relu, bias=sc1[:, pt, 2:3], scale=sc1[:, pt, 1:2])\
                   .then_inc(s_affine1, 1)

            def finish_q1(t):
                act.wait_ge(s_x_rounded, at(t + 1))
                if due(2 * t):
                    act.wait_ge(s_q1T_turned, at(2 * t))
                act.activation(q1[:, :], xw[:, :], ACT.Copy, bias=-(ROUND + ZC)).then_inc(s_q1_ready, 1)

            def take_q1T(t, pt):
                for half in range(2):
                    act.wait_ge(s_q1T_turned, at(2 * t + half + 1))
                    act.activation(q1T[:, pt, half * KC // 2:(half + 1) * KC // 2, :].rearrange("p k m -> p (k m)"),
                                   turnb[half], ACT.Copy).then_inc(s_q1T_ready, 1)

            def split_weights():
                for c in range(4):
                    act.wait_ge(s_a_turned, at(c + 1))
                    act.activation(WT[:, GK * c:GK * (c + 1), 0:ER], turn[c % 2][:, :].rearrange("p (k m) -> p k m", k=GK),
                                   ACT.Copy).then_inc(s_a_high, 1)
                act.wait_ge(s_r_turned, 1)
                act.activation(WT[:, :, ER:WC], wp[:, 0:KC * E].rearrange("p (k m) -> p k m", k=KC),
                               ACT.Copy).then_inc(s_r_high, 1)
                for c in range(4):
                    act.wait_ge(s_b_turned, at(c + 1))
                    act.activation(b_raw.rearrange("e (p j) -> e j p", j=KC)[:, 4 * c:4 * c + 4, :],
                                   turn[c % 2][:, :].rearrange("e (j p) -> e j p", j=4), ACT.Copy).then_inc(s_b_raw, 1)

            act.wait_ge(s_par_ready, 1)
            affine_x(0, 0)
            affine_ctx(0)
            finish_q1(0)
            affine_ctx(1)
            take_q1T(0, 0)
            split_weights()
            for piece in range(2, EARLY - PIECES):
                affine_ctx(piece)

            def period(t, pt):
                if has(t, -1):
                    if due(t):
                        act.wait_ge(s_norm2, at(t))
                    if due(4 * (t - 1)):
                        act.wait_ge(s_y_turned, at(4 * (t - 1)))
                    if has(t, -1) and (not isinstance(t, int) or t <= T):
                        act.activation(y[:, :], xcol(t - 1, 0, D), ACT.Identity, bias=sc2[:, 1 - pt, 2:3],
                                       scale=sc2[:, 1 - pt, 1:2]).then_inc(s_y_ready, 1)
                if isinstance(t, int) and t == 0:
                    for piece in range(EARLY - PIECES, EARLY):
                        affine_ctx(piece)
                if isinstance(t, int) and t == TB:
                    for piece in range(EARLY + TB, EARLY + TB + PIECES):
                        affine_ctx(piece)
                if has(t, 1):
                    affine_x(t + 1, 1 - pt)
                if has(t, -2):
                    if due(t - 1):
                        act.wait_ge(s_wh_turned, at(t - 1))
                    act.activation(whT[:, :, :].rearrange("p a m -> p (a m)"), wph[:, 0:2 * P], ACT.Copy)\
                       .then_inc(s_whT_ready, 1)
                if isinstance(t, int):
                    if t < TB:
                        affine_ctx(EARLY + t)
                    if t == TB:
                        for piece in range(EARLY + TB + PIECES, 2 * EARLY):
                            affine_ctx(piece)
                elif batch0[0]:
                    affine_ctx(EARLY + t, pt)
                if has(t, 1):
                    finish_q1(t + 1)
                if has(t, -1):
                    for g in range(4):
                        act.wait_ge(s_y_turned, at(4 * (t - 1) + g + 1))
                        act.activation(yhi[:, g % 2, :], turn[g % 2][:, :], ACT.Copy).then_inc(s_y_high, 1)
                if has(t, 1):
                    take_q1T(t + 1, 1 - pt)

            batch0 = [True]
            period(0, 0)
            period(1, 1)
            with act.Fori(0, TB // 2 - 1) as pair:
                t = Count(pair, 2, 2)
                period(t, 0)
                period(t + 1, 1)
            batch0[0] = False
            period(TB, 0)
            period(TB + 1, 1)
            with act.Fori(0, (T - TB) // 2 - 2) as pair:
                t = Count(pair, 2, TB + 2)
                period(t, 0)
                period(t + 1, 1)
            for t in range(T - 2, T + 2):
                period(t, t % 2)

        @block_.vector
        def _(dve):
            dve.wait_ge(s_par_loaded, 16 * 6)
            dve.reciprocal(inv[:, :], par[:, 0:2]).then_inc(s_inv_done, 1)
            dve.wait_ge(s_inv_done, 1)
            dve.tensor_scalar(ninv[:, :], inv[:, 0:1], -1.0, None, ALU.mult).then_inc(s_par_ready, 1)
            dve.tensor_scalar(dz[:, :], par[:, 2:4], -1.0, ZC, ALU.mult, ALU.add).then_inc(s_dz_done, 1)
            dve.tensor_scalar(nz[:, :], par[:, 2:4], ZC, None, ALU.not_equal).then_inc(s_nz_done, 1)
            dve.wait_ge(s_nz_done, 1)
            dve.tensor_tensor(flag[:, :], nz[:, 0:1], nz[:, 1:2], ALU.add).then_inc(s_flag_ready, 1)
            dve.wait_ge(s_tanh_done, 1)
            dve.tensor_tensor(c12[:, 0:1], par[:, 0:1], par[:, 1:2], ALU.mult).then_inc(s_s12_done, 1)
            dve.wait_ge(s_s12_done, 1)
            dve.tensor_tensor(cc[:, :], c12[:, 0:1], th[:, 0:1], ALU.mult).then_inc(s_cc_done, 1)
            dve.wait_ge(s_cc_done, 1)
            dve.wait_ge(s_dz_done, 1)
            dve.tensor_scalar(cd[:, :], dz[:, :], cc[:, :], None, ALU.mult).then_inc(s_cd_done, 1)
            dve.wait_ge(s_cd_done, 1)
            dve.tensor_scalar(kdd[:, 0:1], cd[:, 0:1], dz[:, 1:2], float(CTX), ALU.mult, ALU.mult).then_inc(s_kdd_done, 1)
            dve.wait_ge(s_kdd_done, 1)
            dve.wait_ge(s_flag_ready, 1)
            other_zp = dve.value_load(flag[0:1, 0:1].bitcast(i32))

            def stats1(t, pt):
                dve.wait_ge(s_x_loaded[pt], at(16 * (half(t) + 1)))
                dve.sem_inc(s_passed, 1)
                for nb in range(NB):
                    dve.bn_stats(bn1[:, nb, :], xcol(t, nb * NW, (nb + 1) * NW)).then_inc(s_bn1_done, 1)
                dve.wait_ge(s_bn1_done, at(NB * (t + 1)))
                if due(t - 1):
                    dve.wait_ge(s_norm1, at(t - 1))
                dve.sem_inc(s_passed, 1)
                dve.bn_aggr(mv1[:, pt, :], bn1[:, :, :].rearrange("p a b -> p (a b)")).then_inc(s_stats1, 1)

            def round_x(t):
                dve.wait_ge(s_affine1, at(t + 1))
                dve.tensor_scalar(xw[:, :], xw[:, :], QMAX, ROUND, ALU.min, ALU.add).then_inc(s_x_rounded, 1)

            def round_ctx(piece, s=None, dst=None):
                if s is None:
                    s, block, q = stage_of(piece), piece // PIECES, piece % PIECES
                    dst = q2[:, slot(block), q * PK:(q + 1) * PK, :].rearrange("p k n -> p (k n)")
                    if block >= SLOTS:
                        dve.wait_ge(s_main_done, at(NB * (TB - 1) + slot(block) + 1))
                    elif block >= SLOTS - 2:
                        dve.wait_ge(s_weights_ready, 1)
                dve.wait_ge(s_ctx_affine, at(piece + 1))
                dve.tensor_scalar(stage[:, s, :], stage[:, s, :], QMAX, ROUND, ALU.min, ALU.add)\
                   .then_inc(s_ctx_rounded, 1)
                dve.wait_ge(s_ctx_rounded, at(piece + 1))
                dve.tensor_scalar(dst, stage[:, s, :], ROUND + ZC, None, ALU.subtract).then_inc(s_ctx_ready, 1)

            def scale_of(dst, src, step):
                dve.tensor_reduce(dst[:, 0:1], src, AX.X, ALU.max, apply_absolute_value=True).then_inc(step, 1)
                dve.wait_ge(step, 1)
                dve.tensor_scalar(dst[:, 1:2], dst[:, 0:1], TINY, None, ALU.max).then_inc(step, 1)
                dve.wait_ge(step, 2)
                dve.reciprocal(dst[:, 2:3], dst[:, 1:2]).then_inc(step, 1)
                dve.wait_ge(step, 3)
                dve.tensor_scalar(dst[:, 3:4], dst[:, 2:3], WS, None, ALU.mult).then_inc(step, 1)
                dve.wait_ge(step, 4)

            def scale_weights():
                dve.wait_ge(s_a_loaded, 16)
                scale_of(wmax, a_nat, s_wmax_step)
                dve.tensor_scalar(a_nat, a_nat, wmax[:, 3:4], None, ALU.mult).then_inc(s_a_scaled, 1)
                dve.wait_ge(s_r_loaded, 16)
                scale_of(rmax, r_nat, s_rmax_step)
                dve.tensor_scalar(r_nat, r_nat, rmax[:, 3:4], None, ALU.mult).then_inc(s_r_scaled, 1)

            def split_weights():
                for c in range(4):
                    dve.wait_ge(s_a_high, at(c + 1))
                    dve.tensor_tensor(WT[:, GK * c:GK * (c + 1), WC:WC + ER],
                                      turn[c % 2][:, :].rearrange("p (k m) -> p k m", k=GK),
                                      WT[:, GK * c:GK * (c + 1), 0:ER], ALU.subtract).then_inc(s_a_low, 1)
                dve.wait_ge(s_r_high, 1)
                dve.tensor_tensor(WT[:, :, WC + ER:2 * WC], wp[:, 0:KC * E].rearrange("p (k m) -> p k m", k=KC),
                                  WT[:, :, ER:WC], ALU.subtract).then_inc(s_r_low, 1)
                dve.wait_ge(s_b_raw, 4)
                scale_of(bmax, b_raw, s_bmax_step)
                dve.tensor_scalar(BT[:, 0, :], b_raw, bmax[:, 3:4], None, ALU.mult).then_inc(s_b_high, 1)
                dve.wait_ge(s_b_high, 1)
                dve.scalar_tensor_tensor(out=BT[:, 1, :], in0=b_raw, scalar=bmax[:, 3:4], in1=BT[:, 0, :],
                                         op0=ALU.mult, op1=ALU.subtract).then_inc(s_weights_ready, 1)
                dve.tensor_scalar(wsc[:, 0:1], wmax[:, 1:2], 1.0 / (WS * YS), None, ALU.mult).then_inc(s_wsc_step, 1)
                dve.wait_ge(s_wsc_step, 1)
                dve.tensor_scalar(wsc[:, 1:2], bmax[:, 1:2], wsc[:, 0:1], 1.0 / WS, ALU.mult, ALU.mult)\
                   .then_inc(s_wsc_step, 1)
                dve.tensor_scalar(rsc[:, :], rmax[:, 1:2], 1.0 / (WS * YS), None, ALU.mult).then_inc(s_wsc_step, 1)
                dve.wait_ge(s_wsc_step, 3)
                dve.wait_ge(s_idf_made, 1)
                dve.tensor_scalar(diag[:, :], idf[:, :], wsc[:, 1:2], None, ALU.mult).then_inc(s_diag_ready, 1)
                dve.tensor_scalar(diag8[:, :], idf[0:E, 0:E], rsc[:, :], None, ALU.mult).then_inc(s_diag_ready, 1)
                dve.wait_ge(s_scales_spread, 1)
                dve.tensor_copy(wscale[:, :], hp[:, 0:WC]).then_inc(s_wscale_ready, 1)

            def column_terms(b, nb):
                with dve.If(other_zp != 0):
                    dve.wait_ge(s_colsum_done, at(NB * b + nb + 1))
                    dve.tensor_scalar(corr[:, nb * NW:(nb + 1) * NW], wp[:, :], cd[:, 0:1], None, ALU.mult)\
                       .then_inc(s_corr_ready, 1)
                    dve.wait_ge(s_corr_ready, at(NB * b + nb + 1))
                    dve.sem_inc(s_passed, 1)
                    dve.nop()

            def row_term(t, pt):
                with dve.If(other_zp != 0):
                    dve.wait_ge(s_q1_ready, at(t + 1))
                    dve.tensor_reduce(rowc[:, pt, 0:1], q1[:, :], AX.X, ALU.add).then_inc(s_rowsum_done, 1)
                    dve.wait_ge(s_rowsum_done, at(t + 1))
                    dve.tensor_scalar(rowc[:, pt, 1:2], rowc[:, pt, 0:1], cd[:, 1:2], kdd[:, 0:1], ALU.mult, ALU.add)\
                       .then_inc(s_rowc_ready, 1)
                    dve.wait_ge(s_rowc_ready, at(t + 1))
                    dve.sem_inc(s_passed, 1)
                    dve.nop()

            def add_main(t, pt, nb):
                c0, c1 = nb * NW, (nb + 1) * NW
                with dve.If(other_zp != 0):
                    dve.scalar_tensor_tensor(out=xcol(t, c0, c1), in0=xcol(t, c0, c1), scalar=rowc[:, pt, 1:2],
                                             in1=corr[:, c0:c1], op0=ALU.add, op1=ALU.add).then_inc(s_terms_added, 1)
                    dve.wait_ge(s_terms_added, at(NB * t + nb + 1))
                    dve.sem_inc(s_passed, 1)
                    dve.nop()
                dve.wait_ge(s_main_done, at(NB * t + nb + 1))
                dve.scalar_tensor_tensor(out=xcol(t, c0, c1), in0=mainp[nb % 2][:, :], scalar=cc[:, :],
                                         in1=xcol(t, c0, c1), op0=ALU.mult, op1=ALU.add).then_inc(s_main_added, 1)
                dve.wait_ge(s_main_added, at(NB * t + nb + 1))
                dve.sem_inc(s_passed, 1)
                dve.bn_stats(bn2[:, nb, :], xcol(t, c0, c1)).then_inc(s_bn2_done, 1)

            def gate(t, pt):
                n = t + 1
                dve.wait_ge(s_h_done, at(n))
                dve.tensor_copy(hs[:, :], hp[:, WC:2 * WC]).then_inc(s_hs_done, 1)
                dve.wait_ge(s_hs_done, at(n))
                dve.tensor_tensor(hl[:, :], hp[:, 0:WC], hs[:, :], ALU.add).then_inc(s_h_read, 1)
                dve.wait_ge(s_h_read, at(n))
                dve.tensor_tensor(hl[:, :], hl[:, :], wscale[:, :], ALU.mult).then_inc(s_hl_done, 1)
                dve.wait_ge(s_hl_done, at(n))
                dve.sem_inc(s_passed, 1)
                dve.max(top8[:, :], hl[:, ER:WC]).then_inc(s_top_done, 1)
                dve.wait_ge(s_top_done, at(n))
                dve.sem_inc(s_passed, 1)
                dve.max_index(idx8[:, :], top8[:, :], hl[:, ER:WC]).then_inc(s_idx_done, 1)
                dve.wait_ge(s_idx_done, at(n))
                dve.tensor_copy(idxf[:, :], idx8[:, 0:1]).then_inc(s_idxf_done, 1)
                dve.wait_ge(s_idxf_done, at(n))
                dve.tensor_scalar(pick[:, :], eid[:, :], idxf[:, :], top8[:, 0:1], ALU.is_equal, ALU.mult)\
                   .then_inc(s_pick_done, 1)
                dve.wait_ge(s_pick_done, at(n))
                dve.tensor_tensor(wh[:, :], hl[:, 0:ER], pick[:, :], ALU.mult).then_inc(s_wh_done, 1)
                dve.wait_ge(s_wh_done, at(n))
                dve.tensor_reduce(am[:, 0:1], wh[:, :], AX.X, ALU.max, apply_absolute_value=True).then_inc(s_am_done, 1)
                dve.wait_ge(s_am_done, at(n))
                dve.tensor_scalar(am[:, 1:2], am[:, 0:1], TINY, None, ALU.max).then_inc(s_floor_done, 1)
                dve.wait_ge(s_floor_done, at(n))
                dve.reciprocal(am[:, 2:3], am[:, 1:2]).then_inc(s_rec_done, 1)
                dve.tensor_scalar(tsc[:, pt:pt + 1], am[:, 1:2], th[:, 1:2], 1.0 / WS, ALU.mult, ALU.mult)\
                   .then_inc(s_tsc_done, 1)
                dve.wait_ge(s_rec_done, at(n))
                dve.tensor_scalar(am[:, 3:4], am[:, 2:3], WS, None, ALU.mult).then_inc(s_fac_done, 1)
                dve.wait_ge(s_fac_done, at(n))
                dve.tensor_scalar(whs[:, 0, :], wh[:, :], am[:, 3:4], None, ALU.mult).then_inc(s_wh_high, 1)
                dve.wait_ge(s_wh_high, at(n))
                dve.scalar_tensor_tensor(out=whs[:, 1, :], in0=wh[:, :], scalar=am[:, 3:4], in1=whs[:, 0, :],
                                         op0=ALU.mult, op1=ALU.subtract).then_inc(s_wh_ready, 1)
                dve.wait_ge(s_tsc_done, at(n))

            stats1(0, 0)
            round_x(0)
            round_ctx(0)
            round_ctx(1)
            scale_weights()
            split_weights()
            for piece in range(2, EARLY - PIECES):
                round_ctx(piece)
            dve.wait_ge(s_eid_ready, 1)
            dve.wait_ge(s_wscale_ready, 1)
            row_term(0, 0)

            def period(t, pt, batch0):
                if has(t, -2):
                    gate(t - 2, pt)
                if isinstance(t, int) and t == TB:
                    for piece in range(EARLY + TB, EARLY + TB + PIECES):
                        round_ctx(piece)
                if has(t, 1):
                    stats1(t + 1, 1 - pt)
                first = isinstance(t, int) and t % TB == 0 and t < T
                if isinstance(t, int) and t == 0:
                    for piece in range(EARLY - PIECES, EARLY):
                        round_ctx(piece)
                if first:
                    column_terms(t // TB, 0)
                if has(t, 0):
                    add_main(t, pt, 0)
                if has(t, 1):
                    round_x(t + 1)
                if has(t, -2):
                    for g in range(NB):
                        dve.wait_ge(s_out_done, at(NB * (t - 2) + g + 1))
                        dve.scalar_tensor_tensor(out=xcol(t - 2, g * NW, (g + 1) * NW), in0=outp[g % 2][:, :],
                                                 scalar=tsc[:, pt:pt + 1], in1=xcol(t - 2, g * NW, (g + 1) * NW),
                                                 op0=ALU.mult, op1=ALU.add).then_inc(s_outp_read, 1)
                if isinstance(t, int) and t == TB:
                    for piece in range(EARLY + TB + PIECES, 2 * EARLY):
                        round_ctx(piece)
                if first:
                    column_terms(t // TB, 1)
                if has(t, 0):
                    add_main(t, pt, 1)
                if isinstance(t, int):
                    if t < TB:
                        round_ctx(EARLY + t)
                elif batch0:
                    dst = q2[:, bass.ds(at(t) // PIECES + NB, 1), bass.ds(at(t) % PIECES * PK, PK), :]\
                        .rearrange("p a k n -> p (a k n)")
                    round_ctx(EARLY + t, pt, dst)
                if has(t, -1):
                    for g in range(4):
                        dve.wait_ge(s_y_high, at(4 * (t - 1) + g + 1))
                        dve.tensor_tensor(ylo[:, g % 2, :], turn[g % 2][:, :], yhi[:, g % 2, :], ALU.subtract)\
                           .then_inc(s_y_split, 1)
                if first:
                    column_terms(t // TB, 2)
                if has(t, 0):
                    add_main(t, pt, 2)
                if has(t, 1):
                    row_term(t + 1, 1 - pt)
                if first:
                    column_terms(t // TB, 3)
                if has(t, 0):
                    add_main(t, pt, 3)
                    dve.wait_ge(s_bn2_done, at(NB * (t + 1)))
                    if due(t - 1):
                        dve.wait_ge(s_norm2, at(t - 1))
                    dve.sem_inc(s_passed, 1)
                    dve.bn_aggr(mv2[:, pt, :], bn2[:, :, :].rearrange("p a b -> p (a b)")).then_inc(s_stats2, 1)

            period(0, 0, True)
            period(1, 1, True)
            with dve.Fori(0, TB // 2 - 1) as pair:
                t = Count(pair, 2, 2)
                period(t, 0, True)
                period(t + 1, 1, True)
            period(TB, 0, False)
            period(TB + 1, 1, False)
            with dve.Fori(0, (T - TB) // 2 - 2) as pair:
                t = Count(pair, 2, TB + 2)
                period(t, 0, False)
                period(t + 1, 1, False)
            for t in range(T - 2, T + 2):
                period(t, t % 2, False)

        @block_.tensor
        def _(pe):
            pe.wait_ge(s_flag_ready, 1)
            other_zp = pe.value_load(flag[0:1, 0:1].bitcast(i32))
            pe.wait_ge(s_idf_made, 1)
            pe.wait_ge(s_consts, 4)

            def turn_q1(t, half):
                for k in range(KC // 2):
                    c = half * KC // 2 + k
                    last = pe.transpose(turnb[half][:, k * P:(k + 1) * P], q1[:, c * P:(c + 1) * P], idb[:, :])
                last.then_inc(s_q1T_turned, 1)

            def turn_weights():
                pe.wait_ge(s_a_scaled, 1)
                pe.wait_ge(s_q1T_ready, 2)
                for c in range(4):
                    if c >= 2:
                        pe.wait_ge(s_a_low, at(c - 1))
                    for k in range(GK):
                        last = pe.transpose(turn[c % 2][:, k * P:(k + 1) * P],
                                            a_nat[:, (GK * c + k) * P:(GK * c + k + 1) * P], idf[:, :])
                    last.then_inc(s_a_turned, 1)
                pe.wait_ge(s_r_scaled, 1)
                for k in range(KC):
                    last = pe.transpose(wp[:, k * E:(k + 1) * E], r_nat[:, k * P:(k + 1) * P], idf[0:E, 0:E])
                last.then_inc(s_r_turned, 1)
                pe.wait_ge(s_b_permuted, 1)
                bj = b_perm.rearrange("p (j m) -> p j m", m=ER)
                for c in range(4):
                    if c < 2:
                        pe.wait_ge(s_a_low, at(c + 3))
                    else:
                        pe.wait_ge(s_b_raw, at(c - 1))
                    for j in range(4):
                        last = pe.transpose(turn[c % 2][:, j * P:(j + 1) * P], bj[:, 4 * c + j], idf[:, :])
                    last.then_inc(s_b_turned, 1)
                pe.wait_ge(s_diag_ready, 2)
                pe.matmul(hp[:, 0:ER], onesf[:, :], diag[:, :], start=True, stop=True)
                pe.matmul(hp[:, ER:WC], onesf[0:E, :], diag8[:, :], start=True, stop=True).then_inc(s_scales_spread, 1)

            def column_sums(b, nb):
                with pe.If(other_zp != 0):
                    pe.wait_ge(s_ctx_ready, at(PIECES * (NB * b + nb + 1)))
                    if due(NB * b + nb):
                        pe.wait_ge(s_corr_ready, at(NB * b + nb))
                    if b:
                        pe.wait_ge(s_whT_ready, at(TB - 2))
                    for k in range(KC):
                        last = pe.matmul(wp[:, :], onesb[:, :], q2[:, slot(NB * b + nb), k, :],
                                         start=(k == 0), stop=(k == KC - 1))
                    last.then_inc(s_colsum_done, 1)
                    pe.wait_ge(s_corr_ready, at(NB * b + nb + 1))
                    pe.sem_inc(s_passed, 1)
                    pe.nop()

            def main(t, pt, b, nb, between):
                pe.wait_ge(s_ctx_ready, at(PIECES * (NB * b + nb + 1)))
                if due(NB * t + nb - 1):
                    pe.wait_ge(s_main_added, at(NB * t + nb - 1))
                for run in range(4):
                    for k in range(4 * run, 4 * run + 4):
                        last = pe.matmul(mainp[nb % 2][:, :], q1T[:, pt, k, :], q2[:, slot(NB * b + nb), k, :],
                                         start=(k == 0), stop=(k == KC - 1))
                    if run == 3:
                        last.then_inc(s_main_done, 1)
                    between(run)

            def expert_product(t, g):
                pe.wait_ge(s_outp_read, at(NB * t + g + 1))
                o = outp[g % 2][:, :]
                pe.matmul(o, whT[:, 0, :], BT[:, 0, g * NW:(g + 1) * NW], start=True, stop=False)
                pe.matmul(o, whT[:, 0, :], BT[:, 1, g * NW:(g + 1) * NW], start=False, stop=False)
                pe.matmul(o, whT[:, 1, :], BT[:, 0, g * NW:(g + 1) * NW], start=False, stop=True)\
                  .then_inc(s_out_done, 1)

            def turn_y(t, g):
                if g == 0:
                    pe.wait_ge(s_y_ready, at(t + 1))
                if g >= 2:
                    pe.wait_ge(s_y_split, at(4 * t + g - 1))
                for k in range(GK):
                    c = GK * g + k
                    last = pe.transpose(turn[g % 2][:, k * P:(k + 1) * P], y[:, c * P:(c + 1) * P], idf[:, :])
                last.then_inc(s_y_turned, 1)

            def h_product(t, g):
                if g == 0:
                    if due(t):
                        pe.wait_ge(s_h_read, at(t))
                pe.wait_ge(s_y_split, at(4 * t + g + 1))
                for k in range(GK):
                    c = GK * g + k
                    pe.matmul(hp[:, 0:2 * WC], yhi[:, g % 2, k * P:(k + 1) * P], WT[:, c, :],
                              start=(c == 0), stop=False, skip_group_check=True)
                    last = pe.matmul(hp[:, WC:2 * WC], ylo[:, g % 2, k * P:(k + 1) * P], WT[:, c, 0:WC],
                                     start=False, stop=(c == KC - 1), skip_group_check=True)
                if g == 3:
                    last.then_inc(s_h_done, 1)

            def period(t, pt, b):
                first = isinstance(t, int) and t % TB == 0 and t < T
                live = has(t, 0)

                def unit(nb, between):
                    if first:
                        column_sums(b, nb)
                    if live:
                        main(t, pt, b, nb, between)
                    else:
                        for run in range(4):
                            between(run)

                if live:
                    pe.wait_ge(s_q1T_ready, at(2 * (t + 1)))
                unit(0, lambda run: None)
                if has(t, -2):
                    if due(t - 1):
                        pe.wait_ge(s_wh_ready, at(t - 1))
                    for part in range(2):
                        last = pe.transpose(wph[:, part * P:(part + 1) * P], whs[:, part, :], idh[:, :])
                    last.then_inc(s_wh_turned, 1)

                def with_experts(run):
                    if has(t, -2):
                        if run == 0:
                            if due(t - 1):
                                pe.wait_ge(s_whT_ready, at(t - 1))
                        expert_product(t - 2, run)

                def with_y(run):
                    if has(t, -1):
                        if run >= 1:
                            h_product(t - 1, run - 1)
                        if run < 3:
                            turn_y(t - 1, run + 1)

                def with_q1(run):
                    if has(t, -1) and run == 0:
                        h_product(t - 1, 3)
                    if has(t, 1) and run in (1, 2):
                        if run == 1:
                            pe.wait_ge(s_q1_ready, at(t + 2))
                        if due(4 * (t - 1) + run + 2):
                            pe.wait_ge(s_y_split, at(4 * (t - 1) + run + 2))
                        turn_q1(t + 1, run - 1)

                unit(1, with_experts)
                if has(t, -1):
                    turn_y(t - 1, 0)
                unit(2, with_y)
                unit(3, with_q1)

            pe.wait_ge(s_q1_ready, 1)
            turn_q1(0, 0)
            turn_q1(0, 1)
            turn_weights()
            period(0, 0, 0)
            period(1, 1, 0)
            with pe.Fori(0, TB // 2 - 1) as pair:
                t = Count(pair, 2, 2)
                period(t, 0, 0)
                period(t + 1, 1, 0)
            period(TB, 0, 1)
            period(TB + 1, 1, 1)
            with pe.Fori(0, (T - TB) // 2 - 2) as pair:
                t = Count(pair, 2, TB + 2)
                period(t, 0, 1)
                period(t + 1, 1, 1)
            for t in range(T - 2, T + 2):
                period(t, t % 2, 1)


INS = ['x', 'ctx_4096', 'g_xattn', 'g_ffn', 'L0_xattn_x1_scale', 'L0_xattn_x1_zp', 'L0_xattn_x2_scale',
       'L0_xattn_x2_zp', 'L0_ffn_route_w', 'L0_ffn_A', 'L0_ffn_Bw']


def kernel(**inputs):
    import concourse.bacc as bacc
    from concourse.bass_utils import run_bass_kernel_spmd

    nc = bacc.Bacc("TRN2", target_bir_lowering=False, num_devices=1)
    arrays, args = {}, []
    for name in INS:
        a = np.ascontiguousarray(inputs[name])
        arrays[f"in_{name}"] = a
        args.append(nc.dram_tensor(f"in_{name}", a.shape, mybir.dt.from_np(a.dtype), kind="ExternalInput").ap())
    args.append(nc.dram_tensor("out_0", (B, M, D), mybir.dt.float32, kind="ExternalOutput").ap())
    build(nc, *args)
    r = run_bass_kernel_spmd(nc, [arrays], core_ids=[0])
    return r.results[0]["out_0"]
```

```python
from contextlib import ExitStack

import numpy as np
import concourse.bass as bass
from concourse import mybir

P = 128
B, M, D = 2, 1024, 2048
CTX = 2048
E, R = 8, 16
ER = E * R
TB = M // P
T = B * TB
KC = D // P
NW = 512
NB = D // NW
SLOTS = 6
PIECES = 4
PK = KC // PIECES
XS = 4
WC = ER + E
GK = KC // 4
EPS = 1e-5
QMAX = 255.0
ZC = 128.0
ROUND = 12582912.0
YS = 1024.0
WS = 32768.0
TINY = 1e-30


class Count:

    def __init__(self, reg, step, start):
        self.reg, self.step, self.start = reg, step, start

    def __add__(self, n):
        return Count(self.reg, self.step, self.start + n)

    def __sub__(self, n):
        return self + -n

    def __mul__(self, n):
        return Count(self.reg, self.step * n, self.start * n)

    __radd__, __rmul__ = __add__, __mul__

    def value(self):
        return self.reg * self.step + self.start


def at(n):
    return n if isinstance(n, int) else n.value()


def due(n):
    return not isinstance(n, int) or n > 0


def half(n):
    return n // 2 if isinstance(n, int) else Count(n.reg, n.step // 2, n.start // 2)


def build(nc, x, ctx, g_x, g_f, x1_scale, x1_zp, x2_scale, x2_zp, route_w, A, Bw, out):
    f32, bf16, f16 = mybir.dt.float32, mybir.dt.bfloat16, mybir.dt.float16
    i32, u32 = mybir.dt.int32, mybir.dt.uint32
    ALU = mybir.AluOpType
    ACT = mybir.ActivationFunctionType
    AX = mybir.AxisListType

    x_t = x.rearrange("b (t p) n -> (b t) p n", p=P)
    out_t = out.rearrange("b (t p) n -> (b t) p n", p=P)
    ctx_k = ctx.rearrange("b (c p) n -> b p c n", p=P)
    A_v = A.rearrange("e r d -> (e r) d")
    B_v = Bw.rearrange("e (p j) r -> p e j r", p=P)

    st = ExitStack()
    with st:
        def sb(name, shape, dt):
            return st.enter_context(nc.sbuf_tensor(name, shape, dt))

        def bank(name):
            return st.enter_context(nc.psum_tensor(name, [P, NW], f32))

        def sem(name):
            return st.enter_context(nc.semaphore(name))

        s_x_loaded = [sem("x_loaded0"), sem("x_loaded1")]
        s_ctx_loaded = [sem("ctx_loaded0"), sem("ctx_loaded1")]
        s_par_loaded = sem("par_loaded")
        s_a_loaded = sem("a_loaded")
        s_r_loaded = sem("r_loaded")
        s_b_loaded = sem("b_loaded")
        s_stored = sem("stored")
        s_id_zero = sem("id_zero")
        s_idf_made = sem("idf_made")
        s_consts = sem("consts")
        s_mexp_set = sem("mexp_set")
        s_eid_made = sem("eid_made")
        s_eid_ready = sem("eid_ready")
        s_inv_done = sem("inv_done")
        s_par_ready = sem("par_ready")
        s_dz_done = sem("dz_done")
        s_nz_done = sem("nz_done")
        s_flag_ready = sem("flag_ready")
        s_tanh_done = sem("tanh_done")
        s_s12_done = sem("s12_done")
        s_cc_done = sem("cc_done")
        s_cd_done = sem("cd_done")
        s_kdd_done = sem("kdd_done")
        s_wmax_step = sem("wmax_step")
        s_rmax_step = sem("rmax_step")
        s_bmax_step = sem("bmax_step")
        s_a_scaled = sem("a_scaled")
        s_r_scaled = sem("r_scaled")
        s_a_turned = sem("a_turned")
        s_r_turned = sem("r_turned")
        s_a_high = sem("a_high")
        s_r_high = sem("r_high")
        s_a_low = sem("a_low")
        s_r_low = sem("r_low")
        s_b_permuted = sem("b_permuted")
        s_b_turned = sem("b_turned")
        s_b_raw = sem("b_raw")
        s_b_high = sem("b_high")
        s_weights_ready = sem("weights_ready")
        s_wsc_step = sem("wsc_step")
        s_diag_ready = sem("diag_ready")
        s_scales_spread = sem("scales_spread")
        s_wscale_ready = sem("wscale_ready")
        s_ctx_affine = sem("ctx_affine")
        s_ctx_rounded = sem("ctx_rounded")
        s_ctx_ready = sem("ctx_ready")
        s_bn1_done = sem("bn1_done")
        s_stats1 = sem("stats1")
        s_ve1_done = sem("ve1_done")
        s_rs1_done = sem("rs1_done")
        s_na1_done = sem("na1_done")
        s_norm1 = sem("norm1")
        s_affine1 = sem("affine1")
        s_x_rounded = sem("x_rounded")
        s_q1_ready = sem("q1_ready")
        s_q1T_turned = sem("q1T_turned")
        s_q1T_ready = sem("q1T_ready")
        s_main_done = sem("main_done")
        s_main_added = sem("main_added")
        s_bn2_done = sem("bn2_done")
        s_stats2 = sem("stats2")
        s_ve2_done = sem("ve2_done")
        s_rs2_done = sem("rs2_done")
        s_na2_done = sem("na2_done")
        s_norm2 = sem("norm2")
        s_y_ready = sem("y_ready")
        s_y_turned = sem("y_turned")
        s_y_high = sem("y_high")
        s_y_split = sem("y_split")
        s_h_done = sem("h_done")
        s_hs_done = sem("hs_done")
        s_h_read = sem("h_read")
        s_hl_done = sem("hl_done")
        s_top_done = sem("top_done")
        s_idx_done = sem("idx_done")
        s_idxf_done = sem("idxf_done")
        s_pick_done = sem("pick_done")
        s_wh_done = sem("wh_done")
        s_am_done = sem("am_done")
        s_floor_done = sem("floor_done")
        s_rec_done = sem("rec_done")
        s_tsc_done = sem("tsc_done")
        s_fac_done = sem("fac_done")
        s_wh_high = sem("wh_high")
        s_wh_ready = sem("wh_ready")
        s_wh_turned = sem("wh_turned")
        s_whT_ready = sem("whT_ready")
        s_out_done = sem("out_done")
        s_outp_read = sem("outp_read")
        s_colsum_done = sem("colsum_done")
        s_corr_ready = sem("corr_ready")
        s_rowsum_done = sem("rowsum_done")
        s_rowc_ready = sem("rowc_ready")
        s_terms_added = sem("terms_added")
        s_passed = sem("passed")

        q2 = sb("q2", [P, SLOTS, KC, NW], bf16)
        xs = sb("xs", [P, XS, D], f32)
        q1 = sb("q1", [P, D], bf16)
        q1T = sb("q1T", [P, 2, KC, P], bf16)
        xw = sb("xw", [P, D], f32)
        stage = sb("stage", [P, 2, PK * NW], f32)
        y = sb("y", [P, D], f32)
        yhi = sb("yhi", [P, 2, GK * P], f16)
        ylo = sb("ylo", [P, 2, GK * P], f16)
        WT = sb("WT", [P, KC, 2 * WC], f16)
        BT = sb("BT", [P, 2, D], f16)
        hs = sb("hs", [P, WC], f32)
        hl = sb("hl", [P, WC], f32)
        wscale = sb("wscale", [P, WC], f32)
        top8 = sb("top8", [P, 8], f32)
        idx8 = sb("idx8", [P, 8], u32)
        idxf = sb("idxf", [P, 1], f32)
        pick = sb("pick", [P, ER], f32)
        wh = sb("wh", [P, ER], f32)
        whs = sb("whs", [P, 2, ER], f16)
        whT = sb("whT", [P, 2, P], f16)
        am = sb("am", [P, 4], f32)
        tsc = sb("tsc", [P, 2], f32)
        eid_i = wh[:, :].bitcast(i32)
        eid = sb("eid", [P, ER], f32)
        idf = sb("idf", [P, P], f32)
        idb = sb("idb", [P, P], bf16)
        idh = sb("idh", [P, P], f16)
        onesf = sb("onesf", [P, P], f32)
        onesb = sb("onesb", [P, P], bf16)
        diag = pick
        diag8 = sb("diag8", [E, E], f32)
        par = sb("par", [P, 8], f32)
        inv = sb("inv", [P, 2], f32)
        ninv = sb("ninv", [P, 1], f32)
        th = sb("th", [P, 2], f32)
        c12 = sb("c12", [P, 2], f32)
        cc = sb("cc", [P, 1], f32)
        dz = sb("dz", [P, 2], f32)
        cd = sb("cd", [P, 2], f32)
        kdd = sb("kdd", [P, 2], f32)
        nz = sb("nz", [P, 2], f32)
        flag = sb("flag", [P, 1], f32)
        mexp = sb("mexp", [P, 1], f32)
        bn1 = sb("bn1", [P, NB, 6], f32)
        bn2 = sb("bn2", [P, NB, 6], f32)
        mv1 = sb("mv1", [P, 2, 2], f32)
        mv2 = sb("mv2", [P, 2, 2], f32)
        ve1 = sb("ve1", [P, 2], f32)
        ve2 = sb("ve2", [P, 2], f32)
        rs1 = sb("rs1", [P, 2], f32)
        rs2 = sb("rs2", [P, 2], f32)
        sc1 = sb("sc1", [P, 2, 3], f32)
        sc2 = sb("sc2", [P, 2, 3], f32)
        rowc = sb("rowc", [P, 2, 2], f32)
        corr = sb("corr", [P, D], f32)
        wmax = sb("wmax", [P, 4], f32)
        rmax = sb("rmax", [E, 4], f32)
        bmax = sb("bmax", [P, 4], f32)
        wsc = sb("wsc", [P, 2], f32)
        rsc = sb("rsc", [E, 1], f32)

        mainp = [bank("main0"), bank("main1")]
        turn = [bank("turn0"), bank("turn1")]
        turnb = [t[:, :].bitcast(bf16) for t in turn]
        hp = bank("hp")
        wp = bank("wp")
        wph = wp[:, :].bitcast(f16)
        outp = [bank("outp0"), bank("outp1")]

        scr = [q2[:, s, :, :].rearrange("p k n -> p (k n)").bitcast(f32) for s in (SLOTS - 2, SLOTS - 1)]
        a_nat, r_nat = scr[0][:, 0:D], scr[0][0:E, D:2 * D]
        b_nat, b_perm = scr[1][:, 0:D], scr[1][:, D:2 * D]
        b_raw = b_nat

        def xcol(t, c0, c1):
            if isinstance(t, int):
                return xs[:, t % XS, c0:c1]
            return xs[:, bass.ds(at(t) % XS, 1), c0:c1].rearrange("p a n -> p (a n)")

        def slot(block):
            return block % SLOTS

        def stage_of(piece):
            return piece % 2

        def schedule(eng, f):
            f(0, 0, True)
            f(1, 1, True)
            with eng.Fori(0, TB // 2 - 2) as pair:
                t = Count(pair, 2, 2)
                f(t, 0, True)
                f(t + 1, 1, True)
            for t in range(TB - 2, TB + 2):
                f(t, t % 2, t < TB)
            with eng.Fori(0, (T - TB) // 2 - 2) as pair:
                t = Count(pair, 2, TB + 2)
                f(t, 0, False)
                f(t + 1, 1, False)
            for t in range(T - 2, T + 2):
                f(t, t % 2, False)

        def has(t, d):
            return not isinstance(t, int) or 0 <= t + d < T

        EARLY = NB * PIECES
        LATE = EARLY + TB
        block_ = st.enter_context(nc.Block())

        @block_.sync
        def _(sp):
            def load_x(t, pt):
                src = x_t[t] if isinstance(t, int) else x_t[bass.ds(at(t), 1)].rearrange("a p n -> p (a n)")
                sp.dma_start(xcol(t, 0, D), src).then_inc(s_x_loaded[pt], 16)

            def load_ctx(piece):
                b, nb, q = piece // (NB * PIECES), piece // PIECES % NB, piece % PIECES
                if due(piece - 1):
                    sp.wait_ge(s_ctx_ready, at(piece - 1))
                sp.dma_start(stage[:, stage_of(piece), :].rearrange("p (c n) -> p c n", c=PK),
                             ctx_k[b, :, q * PK:(q + 1) * PK, nb * NW:(nb + 1) * NW])\
                  .then_inc(s_ctx_loaded[piece % 2], 16)

            for n, v in enumerate((x1_scale, x2_scale, x1_zp, x2_zp, g_x, g_f)):
                sp.dma_start(par[:, n:n + 1], v.partition_broadcast(P)).then_inc(s_par_loaded, 16)
            load_x(0, 0)
            load_ctx(0)
            load_ctx(1)
            sp.dma_start(a_nat, A_v).then_inc(s_a_loaded, 16)
            sp.dma_start(r_nat, route_w).then_inc(s_r_loaded, 16)
            sp.dma_start(b_nat.rearrange("p (e j r) -> p e (j r)", e=E, r=R),
                         B_v.rearrange("p e j r -> p e (j r)")).then_inc(s_b_loaded, 16)
            for piece in range(2, EARLY):
                load_ctx(piece)
                if piece == 2 * PIECES:
                    load_x(1, 1)

            def loop_ctx(t, pt):
                n = t + 1
                sp.wait_ge(s_ctx_ready, at(EARLY + n - 1))
                src = ctx_k[1, :, bass.ds(at(n) % PIECES * PK, PK), bass.ds(at(n) // PIECES * NW, NW)]
                sp.dma_start(stage[:, 1 - pt, :].rearrange("p (c n) -> p c n", c=PK), src)\
                  .then_inc(s_ctx_loaded[1 - pt], 16)

            def period(t, pt, batch0):
                ahead, behind = [], []
                if isinstance(t, int):
                    if t == 0:
                        ahead = [EARLY]
                    if t < TB:
                        ahead = ahead + [EARLY + t + 1]
                    if t == TB - 1:
                        ahead, behind = [LATE, LATE + 1], [LATE + 2, LATE + 3]
                    if t == TB:
                        ahead, behind = [LATE + 4, LATE + 5], [LATE + 6, LATE + 7]
                elif batch0:
                    loop_ctx(t, pt)
                for piece in ahead:
                    load_ctx(piece)
                if has(t, -2):
                    sp.wait_ge(s_outp_read, at(2 + NB * (t - 1)))
                    dst = out_t[t - 2] if isinstance(t, int) else out_t[bass.ds(at(t - 2), 1)].rearrange("a p n -> p (a n)")
                    sp.dma_start(dst, xcol(t - 2, 0, D)).then_inc(s_stored, 16)
                if has(t, 2):
                    if due(16 * (t - 1)):
                        sp.wait_ge(s_stored, at(16 * (t - 1)))
                    load_x(t + 2, pt)
                for piece in behind:
                    load_ctx(piece)

            schedule(sp, period)
            sp.wait_ge(s_stored, at(16 * T))

        @block_.gpsimd
        def _(pool):
            pool.memset(idf[:, :], 0.0).then_inc(s_id_zero, 1)
            pool.sem_inc(s_outp_read, 2)
            pool.memset(onesf[:, :], 1.0).then_inc(s_consts, 1)
            pool.memset(onesb[:, :], 1.0).then_inc(s_consts, 1)
            pool.memset(mexp[:, :], -0.5).then_inc(s_mexp_set, 1)
            pool.iota(eid_i, pattern=[[1, E], [0, R]], base=0, channel_multiplier=0).then_inc(s_eid_made, 1)
            pool.wait_ge(s_id_zero, 1)
            pool.affine_select(out=idf[:, :], in_=idf[:, :], compare_op=ALU.not_equal, fill=1.0, base=0,
                               pattern=[[-1, P]], channel_multiplier=1).then_inc(s_idf_made, 1)
            pool.wait_ge(s_idf_made, 1)
            pool.tensor_copy(idb[:, :], idf[:, :]).then_inc(s_consts, 1)
            pool.tensor_copy(idh[:, :], idf[:, :]).then_inc(s_consts, 1)
            pool.wait_ge(s_eid_made, 1)
            pool.tensor_copy(eid[:, :], eid_i).then_inc(s_eid_ready, 1)

            def first_norm(t, pt):
                pool.wait_ge(s_stats1, at(t + 1))
                pool.sem_inc(s_passed, 1)
                if isinstance(t, int) and t == 0:
                    pool.wait_ge(s_par_ready, 1)
                    pool.wait_ge(s_mexp_set, 1)
                if due(t - 1):
                    pool.wait_ge(s_affine1, at(t - 1))
                pool.sem_inc(s_passed, 1)
                pool.tensor_scalar(ve1[:, pt:pt + 1], mv1[:, pt, 1:2], EPS, None, ALU.add).then_inc(s_ve1_done, 1)
                pool.wait_ge(s_ve1_done, at(t + 1))
                pool.tensor_tensor(rs1[:, pt:pt + 1], ve1[:, pt:pt + 1], mexp[:, :], ALU.pow).then_inc(s_rs1_done, 1)
                pool.wait_ge(s_rs1_done, at(t + 1))
                pool.tensor_tensor(sc1[:, pt, 0:1], rs1[:, pt:pt + 1], ninv[:, :], ALU.mult).then_inc(s_na1_done, 1)
                pool.tensor_tensor(sc1[:, pt, 1:2], rs1[:, pt:pt + 1], inv[:, 0:1], ALU.mult)
                pool.wait_ge(s_na1_done, at(t + 1))
                pool.sem_inc(s_passed, 1)
                pool.tensor_scalar(sc1[:, pt, 2:3], mv1[:, pt, 0:1], sc1[:, pt, 0:1], par[:, 2:3], ALU.mult, ALU.add)\
                    .then_inc(s_norm1, 1)

            def second_norm(t, pt):
                pool.wait_ge(s_stats2, at(t + 1))
                if due(t - 1):
                    pool.wait_ge(s_y_ready, at(t - 1))
                pool.sem_inc(s_passed, 1)
                pool.tensor_scalar(ve2[:, pt:pt + 1], mv2[:, pt, 1:2], EPS, None, ALU.add).then_inc(s_ve2_done, 1)
                pool.wait_ge(s_ve2_done, at(t + 1))
                pool.tensor_tensor(rs2[:, pt:pt + 1], ve2[:, pt:pt + 1], mexp[:, :], ALU.pow).then_inc(s_rs2_done, 1)
                pool.wait_ge(s_rs2_done, at(t + 1))
                pool.sem_inc(s_passed, 1)
                pool.tensor_scalar(sc2[:, pt, 0:1], rs2[:, pt:pt + 1], -YS, None, ALU.mult).then_inc(s_na2_done, 1)
                pool.tensor_scalar(sc2[:, pt, 1:2], rs2[:, pt:pt + 1], YS, None, ALU.mult)
                pool.wait_ge(s_na2_done, at(t + 1))
                pool.tensor_tensor(sc2[:, pt, 2:3], mv2[:, pt, 0:1], sc2[:, pt, 0:1], ALU.mult).then_inc(s_norm2, 1)

            first_norm(0, 0)
            pool.wait_ge(s_b_loaded, 16)
            pool.tensor_copy(b_perm.rearrange("p (j e r) -> p e j r", e=E, r=R),
                             b_nat.rearrange("p (e j r) -> p e j r", e=E, r=R)).then_inc(s_b_permuted, 1)

            def period(t, pt, batch0):
                if has(t, 1):
                    first_norm(t + 1, 1 - pt)
                if has(t, 0):
                    second_norm(t, pt)

            schedule(pool, period)

        @block_.scalar
        def _(act):
            act.wait_ge(s_par_loaded, 16 * 6)
            act.activation(th[:, :], par[:, 4:6], ACT.Tanh).then_inc(s_tanh_done, 1)

            def affine_ctx(piece, n=None):
                s = stage_of(piece) if n is None else n
                act.wait_ge(s_ctx_loaded[s], at(16 * (half(piece) + 1)))
                act.activation(stage[:, s, :], stage[:, s, :], ACT.Relu, bias=par[:, 3:4], scale=inv[:, 1:2])\
                   .then_inc(s_ctx_affine, 1)

            def affine_x(t, pt):
                act.wait_ge(s_norm1, at(t + 1))
                if due(t):
                    act.wait_ge(s_q1_ready, at(t))
                act.activation(xw[:, :], xcol(t, 0, D), ACT.Relu, bias=sc1[:, pt, 2:3], scale=sc1[:, pt, 1:2])\
                   .then_inc(s_affine1, 1)

            def finish_q1(t):
                act.wait_ge(s_x_rounded, at(t + 1))
                if due(2 * t):
                    act.wait_ge(s_q1T_turned, at(2 * t))
                act.activation(q1[:, :], xw[:, :], ACT.Copy, bias=-(ROUND + ZC)).then_inc(s_q1_ready, 1)

            def take_q1T(t, pt):
                for half in range(2):
                    act.wait_ge(s_q1T_turned, at(2 * t + half + 1))
                    act.activation(q1T[:, pt, half * KC // 2:(half + 1) * KC // 2, :].rearrange("p k m -> p (k m)"),
                                   turnb[half], ACT.Copy).then_inc(s_q1T_ready, 1)

            def split_weights():
                for c in range(4):
                    act.wait_ge(s_a_turned, at(c + 1))
                    act.activation(WT[:, GK * c:GK * (c + 1), 0:ER], turn[c % 2][:, :].rearrange("p (k m) -> p k m", k=GK),
                                   ACT.Copy).then_inc(s_a_high, 1)
                act.wait_ge(s_r_turned, 1)
                act.activation(WT[:, :, ER:WC], wp[:, 0:KC * E].rearrange("p (k m) -> p k m", k=KC),
                               ACT.Copy).then_inc(s_r_high, 1)
                for c in range(4):
                    act.wait_ge(s_b_turned, at(c + 1))
                    act.activation(b_raw.rearrange("e (p j) -> e j p", j=KC)[:, 4 * c:4 * c + 4, :],
                                   turn[c % 2][:, :].rearrange("e (j p) -> e j p", j=4), ACT.Copy).then_inc(s_b_raw, 1)

            act.wait_ge(s_par_ready, 1)
            affine_x(0, 0)
            affine_ctx(0)
            finish_q1(0)
            affine_ctx(1)
            take_q1T(0, 0)
            split_weights()
            for piece in range(2, EARLY - PIECES):
                affine_ctx(piece)

            def high_part(t, g):
                act.wait_ge(s_y_turned, at(4 * t + g + 1))
                act.activation(yhi[:, g % 2, :], turn[g % 2][:, :], ACT.Copy).then_inc(s_y_high, 1)

            def period(t, pt, batch0):
                if has(t, -2):
                    if due(t - 1):
                        act.wait_ge(s_wh_turned, at(t - 1))
                    act.activation(whT[:, :, :].rearrange("p a m -> p (a m)"), wph[:, 0:2 * P], ACT.Copy)\
                       .then_inc(s_whT_ready, 1)
                if has(t, -1):
                    if due(t):
                        act.wait_ge(s_norm2, at(t))
                    if due(4 * (t - 1)):
                        act.wait_ge(s_y_turned, at(4 * (t - 1)))
                    act.activation(y[:, :], xcol(t - 1, 0, D), ACT.Identity, bias=sc2[:, 1 - pt, 2:3],
                                   scale=sc2[:, 1 - pt, 1:2]).then_inc(s_y_ready, 1)
                if isinstance(t, int) and t == 0:
                    for piece in range(EARLY - PIECES, EARLY):
                        affine_ctx(piece)
                if isinstance(t, int) and t == TB:
                    affine_ctx(LATE + 4)
                if has(t, 1):
                    affine_x(t + 1, 1 - pt)
                if isinstance(t, int):
                    if t < TB:
                        affine_ctx(EARLY + t)
                    if t == TB:
                        affine_ctx(LATE + 5)
                elif batch0:
                    affine_ctx(EARLY + t, pt)
                if has(t, 1):
                    finish_q1(t + 1)
                if has(t, -1):
                    high_part(t - 1, 0)
                    high_part(t - 1, 1)
                if isinstance(t, int) and t in (TB - 1, TB):
                    affine_ctx(LATE if t < TB else LATE + 6)
                if has(t, -1):
                    high_part(t - 1, 2)
                if isinstance(t, int) and t == TB:
                    affine_ctx(LATE + 7)
                if has(t, -1):
                    high_part(t - 1, 3)
                if isinstance(t, int) and t == TB - 1:
                    affine_ctx(LATE + 1)
                if has(t, 1):
                    take_q1T(t + 1, 1 - pt)
                if isinstance(t, int) and t == TB - 1:
                    affine_ctx(LATE + 2)
                    affine_ctx(LATE + 3)

            schedule(act, period)

        @block_.vector
        def _(dve):
            dve.wait_ge(s_par_loaded, 16 * 6)
            dve.reciprocal(inv[:, :], par[:, 0:2]).then_inc(s_inv_done, 1)
            dve.wait_ge(s_inv_done, 1)
            dve.tensor_scalar(ninv[:, :], inv[:, 0:1], -1.0, None, ALU.mult).then_inc(s_par_ready, 1)
            dve.tensor_scalar(dz[:, :], par[:, 2:4], -1.0, ZC, ALU.mult, ALU.add).then_inc(s_dz_done, 1)
            dve.tensor_scalar(nz[:, :], par[:, 2:4], ZC, None, ALU.not_equal).then_inc(s_nz_done, 1)
            dve.wait_ge(s_nz_done, 1)
            dve.tensor_tensor(flag[:, :], nz[:, 0:1], nz[:, 1:2], ALU.add).then_inc(s_flag_ready, 1)
            dve.wait_ge(s_tanh_done, 1)
            dve.tensor_tensor(c12[:, 0:1], par[:, 0:1], par[:, 1:2], ALU.mult).then_inc(s_s12_done, 1)
            dve.wait_ge(s_s12_done, 1)
            dve.tensor_tensor(cc[:, :], c12[:, 0:1], th[:, 0:1], ALU.mult).then_inc(s_cc_done, 1)
            dve.wait_ge(s_cc_done, 1)
            dve.wait_ge(s_dz_done, 1)
            dve.tensor_scalar(cd[:, :], dz[:, :], cc[:, :], None, ALU.mult).then_inc(s_cd_done, 1)
            dve.wait_ge(s_cd_done, 1)
            dve.tensor_scalar(kdd[:, 0:1], cd[:, 0:1], dz[:, 1:2], float(CTX), ALU.mult, ALU.mult).then_inc(s_kdd_done, 1)
            dve.wait_ge(s_kdd_done, 1)
            dve.wait_ge(s_flag_ready, 1)
            other_zp = dve.value_load(flag[0:1, 0:1].bitcast(i32))

            def stats1(t, pt):
                dve.wait_ge(s_x_loaded[pt], at(16 * (half(t) + 1)))
                dve.sem_inc(s_passed, 1)
                for nb in range(NB):
                    dve.bn_stats(bn1[:, nb, :], xcol(t, nb * NW, (nb + 1) * NW)).then_inc(s_bn1_done, 1)
                dve.wait_ge(s_bn1_done, at(NB * (t + 1)))
                if due(t - 1):
                    dve.wait_ge(s_norm1, at(t - 1))
                dve.sem_inc(s_passed, 1)
                dve.bn_aggr(mv1[:, pt, :], bn1[:, :, :].rearrange("p a b -> p (a b)")).then_inc(s_stats1, 1)

            def round_x(t):
                dve.wait_ge(s_affine1, at(t + 1))
                dve.tensor_scalar(xw[:, :], xw[:, :], QMAX, ROUND, ALU.min, ALU.add).then_inc(s_x_rounded, 1)

            def round_ctx(piece, s=None, dst=None):
                if s is None:
                    s, block, q = stage_of(piece), piece // PIECES, piece % PIECES
                    dst = q2[:, slot(block), q * PK:(q + 1) * PK, :].rearrange("p k n -> p (k n)")
                    if block >= SLOTS:
                        dve.wait_ge(s_main_done, at(NB * (TB - 1) + slot(block) + 1))
                    elif block >= SLOTS - 2:
                        dve.wait_ge(s_weights_ready, 1)
                dve.wait_ge(s_ctx_affine, at(piece + 1))
                dve.tensor_scalar(stage[:, s, :], stage[:, s, :], QMAX, ROUND, ALU.min, ALU.add)\
                   .then_inc(s_ctx_rounded, 1)
                dve.wait_ge(s_ctx_rounded, at(piece + 1))
                dve.tensor_scalar(dst, stage[:, s, :], ROUND + ZC, None, ALU.subtract).then_inc(s_ctx_ready, 1)

            def scale_of(dst, src, step):
                dve.tensor_reduce(dst[:, 0:1], src, AX.X, ALU.max, apply_absolute_value=True).then_inc(step, 1)
                dve.wait_ge(step, 1)
                dve.tensor_scalar(dst[:, 1:2], dst[:, 0:1], TINY, None, ALU.max).then_inc(step, 1)
                dve.wait_ge(step, 2)
                dve.reciprocal(dst[:, 2:3], dst[:, 1:2]).then_inc(step, 1)
                dve.wait_ge(step, 3)
                dve.tensor_scalar(dst[:, 3:4], dst[:, 2:3], WS, None, ALU.mult).then_inc(step, 1)
                dve.wait_ge(step, 4)

            def scale_weights():
                dve.wait_ge(s_a_loaded, 16)
                scale_of(wmax, a_nat, s_wmax_step)
                dve.tensor_scalar(a_nat, a_nat, wmax[:, 3:4], None, ALU.mult).then_inc(s_a_scaled, 1)
                dve.wait_ge(s_r_loaded, 16)
                scale_of(rmax, r_nat, s_rmax_step)
                dve.tensor_scalar(r_nat, r_nat, rmax[:, 3:4], None, ALU.mult).then_inc(s_r_scaled, 1)

            def split_weights():
                for c in range(4):
                    dve.wait_ge(s_a_high, at(c + 1))
                    dve.tensor_tensor(WT[:, GK * c:GK * (c + 1), WC:WC + ER],
                                      turn[c % 2][:, :].rearrange("p (k m) -> p k m", k=GK),
                                      WT[:, GK * c:GK * (c + 1), 0:ER], ALU.subtract).then_inc(s_a_low, 1)
                dve.wait_ge(s_r_high, 1)
                dve.tensor_tensor(WT[:, :, WC + ER:2 * WC], wp[:, 0:KC * E].rearrange("p (k m) -> p k m", k=KC),
                                  WT[:, :, ER:WC], ALU.subtract).then_inc(s_r_low, 1)
                dve.wait_ge(s_b_raw, 4)
                scale_of(bmax, b_raw, s_bmax_step)
                dve.tensor_scalar(BT[:, 0, :], b_raw, bmax[:, 3:4], None, ALU.mult).then_inc(s_b_high, 1)
                dve.wait_ge(s_b_high, 1)
                dve.scalar_tensor_tensor(out=BT[:, 1, :], in0=b_raw, scalar=bmax[:, 3:4], in1=BT[:, 0, :],
                                         op0=ALU.mult, op1=ALU.subtract).then_inc(s_weights_ready, 1)
                dve.tensor_scalar(wsc[:, 0:1], wmax[:, 1:2], 1.0 / (WS * YS), None, ALU.mult).then_inc(s_wsc_step, 1)
                dve.wait_ge(s_wsc_step, 1)
                dve.tensor_scalar(wsc[:, 1:2], bmax[:, 1:2], wsc[:, 0:1], 1.0 / WS, ALU.mult, ALU.mult)\
                   .then_inc(s_wsc_step, 1)
                dve.tensor_scalar(rsc[:, :], rmax[:, 1:2], 1.0 / (WS * YS), None, ALU.mult).then_inc(s_wsc_step, 1)
                dve.wait_ge(s_wsc_step, 3)
                dve.wait_ge(s_idf_made, 1)
                dve.tensor_scalar(diag[:, :], idf[:, :], wsc[:, 1:2], None, ALU.mult).then_inc(s_diag_ready, 1)
                dve.tensor_scalar(diag8[:, :], idf[0:E, 0:E], rsc[:, :], None, ALU.mult).then_inc(s_diag_ready, 1)
                dve.wait_ge(s_scales_spread, 1)
                dve.tensor_copy(wscale[:, :], hp[:, 0:WC]).then_inc(s_wscale_ready, 1)

            def column_terms(b, nb):
                with dve.If(other_zp != 0):
                    dve.wait_ge(s_colsum_done, at(NB * b + nb + 1))
                    dve.tensor_scalar(corr[:, nb * NW:(nb + 1) * NW], wp[:, :], cd[:, 0:1], None, ALU.mult)\
                       .then_inc(s_corr_ready, 1)
                    dve.wait_ge(s_corr_ready, at(NB * b + nb + 1))
                    dve.sem_inc(s_passed, 1)
                    dve.nop()

            def row_term(t, pt):
                with dve.If(other_zp != 0):
                    dve.wait_ge(s_q1_ready, at(t + 1))
                    dve.tensor_reduce(rowc[:, pt, 0:1], q1[:, :], AX.X, ALU.add).then_inc(s_rowsum_done, 1)
                    dve.wait_ge(s_rowsum_done, at(t + 1))
                    dve.tensor_scalar(rowc[:, pt, 1:2], rowc[:, pt, 0:1], cd[:, 1:2], kdd[:, 0:1], ALU.mult, ALU.add)\
                       .then_inc(s_rowc_ready, 1)
                    dve.wait_ge(s_rowc_ready, at(t + 1))
                    dve.sem_inc(s_passed, 1)
                    dve.nop()

            def add_main(t, pt, nb):
                c0, c1 = nb * NW, (nb + 1) * NW
                with dve.If(other_zp != 0):
                    dve.scalar_tensor_tensor(out=xcol(t, c0, c1), in0=xcol(t, c0, c1), scalar=rowc[:, pt, 1:2],
                                             in1=corr[:, c0:c1], op0=ALU.add, op1=ALU.add).then_inc(s_terms_added, 1)
                    dve.wait_ge(s_terms_added, at(NB * t + nb + 1))
                    dve.sem_inc(s_passed, 1)
                    dve.nop()
                dve.wait_ge(s_main_done, at(NB * t + nb + 1))
                dve.scalar_tensor_tensor(out=xcol(t, c0, c1), in0=mainp[nb % 2][:, :], scalar=cc[:, :],
                                         in1=xcol(t, c0, c1), op0=ALU.mult, op1=ALU.add).then_inc(s_main_added, 1)

            def stats2(t, nb):
                dve.wait_ge(s_main_added, at(NB * t + nb + 1))
                dve.sem_inc(s_passed, 1)
                c0, c1 = nb * NW, (nb + 1) * NW
                dve.bn_stats(bn2[:, nb, :], xcol(t, c0, c1)).then_inc(s_bn2_done, 1)

            def gate(t, pt):
                n = t + 1
                dve.wait_ge(s_h_done, at(n))
                dve.tensor_copy(hs[:, :], hp[:, WC:2 * WC]).then_inc(s_hs_done, 1)
                dve.wait_ge(s_hs_done, at(n))
                dve.tensor_tensor(hl[:, :], hp[:, 0:WC], hs[:, :], ALU.add).then_inc(s_h_read, 1)
                dve.wait_ge(s_h_read, at(n))
                dve.tensor_tensor(hl[:, :], hl[:, :], wscale[:, :], ALU.mult).then_inc(s_hl_done, 1)
                dve.wait_ge(s_hl_done, at(n))
                dve.sem_inc(s_passed, 1)
                dve.max(top8[:, :], hl[:, ER:WC]).then_inc(s_top_done, 1)
                dve.wait_ge(s_top_done, at(n))
                dve.sem_inc(s_passed, 1)
                dve.max_index(idx8[:, :], top8[:, :], hl[:, ER:WC]).then_inc(s_idx_done, 1)
                dve.wait_ge(s_idx_done, at(n))
                dve.tensor_copy(idxf[:, :], idx8[:, 0:1]).then_inc(s_idxf_done, 1)
                dve.wait_ge(s_idxf_done, at(n))
                dve.tensor_scalar(pick[:, :], eid[:, :], idxf[:, :], top8[:, 0:1], ALU.is_equal, ALU.mult)\
                   .then_inc(s_pick_done, 1)
                dve.wait_ge(s_pick_done, at(n))
                dve.tensor_tensor(wh[:, :], hl[:, 0:ER], pick[:, :], ALU.mult).then_inc(s_wh_done, 1)
                dve.wait_ge(s_wh_done, at(n))
                dve.tensor_reduce(am[:, 0:1], wh[:, :], AX.X, ALU.max, apply_absolute_value=True).then_inc(s_am_done, 1)
                dve.wait_ge(s_am_done, at(n))
                dve.tensor_scalar(am[:, 1:2], am[:, 0:1], TINY, None, ALU.max).then_inc(s_floor_done, 1)
                dve.wait_ge(s_floor_done, at(n))
                dve.reciprocal(am[:, 2:3], am[:, 1:2]).then_inc(s_rec_done, 1)
                dve.tensor_scalar(tsc[:, pt:pt + 1], am[:, 1:2], th[:, 1:2], 1.0 / WS, ALU.mult, ALU.mult)\
                   .then_inc(s_tsc_done, 1)
                dve.wait_ge(s_rec_done, at(n))
                dve.tensor_scalar(am[:, 3:4], am[:, 2:3], WS, None, ALU.mult).then_inc(s_fac_done, 1)
                dve.wait_ge(s_fac_done, at(n))
                dve.tensor_scalar(whs[:, 0, :], wh[:, :], am[:, 3:4], None, ALU.mult).then_inc(s_wh_high, 1)
                dve.wait_ge(s_wh_high, at(n))
                dve.scalar_tensor_tensor(out=whs[:, 1, :], in0=wh[:, :], scalar=am[:, 3:4], in1=whs[:, 0, :],
                                         op0=ALU.mult, op1=ALU.subtract).then_inc(s_wh_ready, 1)
                dve.wait_ge(s_tsc_done, at(n))
                dve.sem_inc(s_passed, 1)

            stats1(0, 0)
            round_x(0)
            round_ctx(0)
            round_ctx(1)
            scale_weights()
            split_weights()
            for piece in range(2, EARLY - PIECES):
                round_ctx(piece)
            dve.wait_ge(s_eid_ready, 1)
            dve.wait_ge(s_wscale_ready, 1)
            row_term(0, 0)

            def add_experts(t, pt, g):
                dve.wait_ge(s_out_done, at(NB * t + g + 1))
                dve.scalar_tensor_tensor(out=xcol(t, g * NW, (g + 1) * NW), in0=outp[g % 2][:, :],
                                         scalar=tsc[:, pt:pt + 1], in1=xcol(t, g * NW, (g + 1) * NW),
                                         op0=ALU.mult, op1=ALU.add).then_inc(s_outp_read, 1)

            def low_part(t, g):
                dve.wait_ge(s_y_high, at(4 * t + g + 1))
                dve.tensor_tensor(ylo[:, g % 2, :], turn[g % 2][:, :], yhi[:, g % 2, :], ALU.subtract)\
                   .then_inc(s_y_split, 1)

            def period(t, pt, batch0):
                first = isinstance(t, int) and t % TB == 0 and t < T
                at_start, last0 = isinstance(t, int) and t == 0, isinstance(t, int) and t == TB - 1
                at_switch = isinstance(t, int) and t == TB
                here, before, experts, after = has(t, 0), has(t, -1), has(t, -2), has(t, 1)
                if first:
                    column_terms(t // TB, 0)
                if at_switch:
                    round_ctx(LATE + 3)
                if after:
                    stats1(t + 1, 1 - pt)
                if at_start:
                    for piece in range(EARLY - PIECES, EARLY):
                        round_ctx(piece)
                if at_switch:
                    round_ctx(LATE + 4)
                if experts:
                    add_experts(t - 2, pt, 0)
                if here:
                    add_main(t, pt, 0)
                if experts:
                    add_experts(t - 2, pt, 1)
                if first:
                    column_terms(t // TB, 1)
                if here:
                    stats2(t, 0)
                if after:
                    round_x(t + 1)
                if isinstance(t, int):
                    if t < TB:
                        round_ctx(EARLY + t)
                    if t == TB:
                        round_ctx(LATE + 5)
                elif batch0:
                    dst = q2[:, bass.ds(at(t) // PIECES + NB, 1), bass.ds(at(t) % PIECES * PK, PK), :]\
                        .rearrange("p a k n -> p (a k n)")
                    round_ctx(EARLY + t, pt, dst)
                if experts:
                    add_experts(t - 2, pt, 2)
                if before:
                    low_part(t - 1, 0)
                if experts:
                    add_experts(t - 2, pt, 3)
                if here:
                    add_main(t, pt, 1)
                if first:
                    column_terms(t // TB, 2)
                if before:
                    low_part(t - 1, 1)
                if here:
                    stats2(t, 1)
                if last0:
                    round_ctx(LATE)
                if at_switch:
                    round_ctx(LATE + 6)
                if before:
                    low_part(t - 1, 2)
                if at_switch:
                    round_ctx(LATE + 7)
                if before:
                    low_part(t - 1, 3)
                if last0:
                    round_ctx(LATE + 1)
                if first:
                    column_terms(t // TB, 3)
                if here:
                    add_main(t, pt, 2)
                if after:
                    row_term(t + 1, 1 - pt)
                if here:
                    stats2(t, 2)
                if before:
                    gate(t - 1, 1 - pt)
                if last0:
                    round_ctx(LATE + 2)
                if here:
                    add_main(t, pt, 3)
                    stats2(t, 3)
                    dve.wait_ge(s_bn2_done, at(NB * (t + 1)))
                    if due(t - 1):
                        dve.wait_ge(s_norm2, at(t - 1))
                    dve.sem_inc(s_passed, 1)
                    dve.bn_aggr(mv2[:, pt, :], bn2[:, :, :].rearrange("p a b -> p (a b)")).then_inc(s_stats2, 1)

            schedule(dve, period)

        @block_.tensor
        def _(pe):
            pe.wait_ge(s_flag_ready, 1)
            other_zp = pe.value_load(flag[0:1, 0:1].bitcast(i32))
            pe.wait_ge(s_idf_made, 1)
            pe.wait_ge(s_consts, 4)

            def turn_q1(t, half):
                for k in range(KC // 2):
                    c = half * KC // 2 + k
                    last = pe.transpose(turnb[half][:, k * P:(k + 1) * P], q1[:, c * P:(c + 1) * P], idb[:, :])
                last.then_inc(s_q1T_turned, 1)

            def turn_weights():
                pe.wait_ge(s_a_scaled, 1)
                pe.wait_ge(s_q1T_ready, 2)
                for c in range(4):
                    if c >= 2:
                        pe.wait_ge(s_a_low, at(c - 1))
                    for k in range(GK):
                        last = pe.transpose(turn[c % 2][:, k * P:(k + 1) * P],
                                            a_nat[:, (GK * c + k) * P:(GK * c + k + 1) * P], idf[:, :])
                    last.then_inc(s_a_turned, 1)
                pe.wait_ge(s_r_scaled, 1)
                for k in range(KC):
                    last = pe.transpose(wp[:, k * E:(k + 1) * E], r_nat[:, k * P:(k + 1) * P], idf[0:E, 0:E])
                last.then_inc(s_r_turned, 1)
                pe.wait_ge(s_b_permuted, 1)
                bj = b_perm.rearrange("p (j m) -> p j m", m=ER)
                for c in range(4):
                    if c < 2:
                        pe.wait_ge(s_a_low, at(c + 3))
                    else:
                        pe.wait_ge(s_b_raw, at(c - 1))
                    for j in range(4):
                        last = pe.transpose(turn[c % 2][:, j * P:(j + 1) * P], bj[:, 4 * c + j], idf[:, :])
                    last.then_inc(s_b_turned, 1)
                pe.wait_ge(s_diag_ready, 2)
                pe.matmul(hp[:, 0:ER], onesf[:, :], diag[:, :], start=True, stop=True)
                pe.matmul(hp[:, ER:WC], onesf[0:E, :], diag8[:, :], start=True, stop=True).then_inc(s_scales_spread, 1)

            def column_sums(b, nb):
                with pe.If(other_zp != 0):
                    pe.wait_ge(s_ctx_ready, at(PIECES * (NB * b + nb + 1)))
                    if due(NB * b + nb):
                        pe.wait_ge(s_corr_ready, at(NB * b + nb))
                    if b:
                        pe.wait_ge(s_whT_ready, TB - 2 if nb == 0 else TB - 1)
                    for k in range(KC):
                        last = pe.matmul(wp[:, :], onesb[:, :], q2[:, slot(NB * b + nb), k, :],
                                         start=(k == 0), stop=(k == KC - 1))
                    last.then_inc(s_colsum_done, 1)
                    pe.wait_ge(s_corr_ready, at(NB * b + nb + 1))
                    pe.sem_inc(s_passed, 1)
                    pe.nop()

            def main(t, pt, b, nb, between):
                pe.wait_ge(s_ctx_ready, at(PIECES * (NB * b + nb + 1)))
                if due(NB * t + nb - 1):
                    pe.wait_ge(s_main_added, at(NB * t + nb - 1))
                for run in range(4):
                    for k in range(4 * run, 4 * run + 4):
                        last = pe.matmul(mainp[nb % 2][:, :], q1T[:, pt, k, :], q2[:, slot(NB * b + nb), k, :],
                                         start=(k == 0), stop=(k == KC - 1))
                    if run == 3:
                        last.then_inc(s_main_done, 1)
                    between(run)

            def expert_product(t, g):
                pe.wait_ge(s_outp_read, at(NB * t + g + 1))
                o = outp[g % 2][:, :]
                pe.matmul(o, whT[:, 0, :], BT[:, 0, g * NW:(g + 1) * NW], start=True, stop=False)
                pe.matmul(o, whT[:, 0, :], BT[:, 1, g * NW:(g + 1) * NW], start=False, stop=False)
                pe.matmul(o, whT[:, 1, :], BT[:, 0, g * NW:(g + 1) * NW], start=False, stop=True)\
                  .then_inc(s_out_done, 1)

            def turn_y(t, g):
                if g == 0:
                    pe.wait_ge(s_y_ready, at(t + 1))
                if g >= 2:
                    pe.wait_ge(s_y_split, at(4 * t + g - 1))
                for k in range(GK):
                    c = GK * g + k
                    last = pe.transpose(turn[g % 2][:, k * P:(k + 1) * P], y[:, c * P:(c + 1) * P], idf[:, :])
                last.then_inc(s_y_turned, 1)

            def h_product(t, g):
                if g == 0:
                    if due(t):
                        pe.wait_ge(s_h_read, at(t))
                pe.wait_ge(s_y_split, at(4 * t + g + 1))
                for k in range(GK):
                    c = GK * g + k
                    pe.matmul(hp[:, 0:2 * WC], yhi[:, g % 2, k * P:(k + 1) * P], WT[:, c, :],
                              start=(c == 0), stop=False, skip_group_check=True)
                    last = pe.matmul(hp[:, WC:2 * WC], ylo[:, g % 2, k * P:(k + 1) * P], WT[:, c, 0:WC],
                                     start=False, stop=(c == KC - 1), skip_group_check=True)
                if g == 3:
                    last.then_inc(s_h_done, 1)

            def period(t, pt, batch0):
                first = isinstance(t, int) and t % TB == 0 and t < T
                before, experts, after = has(t, -1), has(t, -2), has(t, 1)
                b = 0 if batch0 else 1

                def unit(nb, between):
                    if first:
                        column_sums(b, nb)
                    if has(t, 0):
                        main(t, pt, b, nb, between)
                    else:
                        for run in range(4):
                            between(run)

                def unit0(run):
                    if experts and run == 0:
                        if due(t - 1):
                            pe.wait_ge(s_wh_ready, at(t - 1))
                        for part in range(2):
                            last = pe.transpose(wph[:, part * P:(part + 1) * P], whs[:, part, :], idh[:, :])
                        last.then_inc(s_wh_turned, 1)
                    if experts and run == 1:
                        if due(t - 1):
                            pe.wait_ge(s_whT_ready, at(t - 1))
                        expert_product(t - 2, 0)
                    if experts and run == 3:
                        expert_product(t - 2, 1)

                def unit1(run):
                    if experts and run == 1:
                        expert_product(t - 2, 2)
                    if before and run == 2:
                        turn_y(t - 1, 0)
                    if experts and run == 3:
                        expert_product(t - 2, 3)
                    if before and run == 3:
                        turn_y(t - 1, 1)

                def unit2(run):
                    if before:
                        h_product(t - 1, run)
                        if run < 2:
                            turn_y(t - 1, run + 2)

                def unit3(run):
                    if after and run < 2:
                        if run == 0:
                            pe.wait_ge(s_q1_ready, at(t + 2))
                        if due(4 * (t - 1) + run + 3):
                            pe.wait_ge(s_y_split, at(4 * (t - 1) + run + 3))
                        turn_q1(t + 1, run)

                if has(t, 0):
                    pe.wait_ge(s_q1T_ready, at(2 * (t + 1)))
                unit(0, unit0)
                unit(1, unit1)
                unit(2, unit2)
                unit(3, unit3)

            pe.wait_ge(s_q1_ready, 1)
            turn_q1(0, 0)
            turn_q1(0, 1)
            turn_weights()
            schedule(pe, period)


INS = ['x', 'ctx_4096', 'g_xattn', 'g_ffn', 'L0_xattn_x1_scale', 'L0_xattn_x1_zp', 'L0_xattn_x2_scale',
       'L0_xattn_x2_zp', 'L0_ffn_route_w', 'L0_ffn_A', 'L0_ffn_Bw']


def kernel(**inputs):
    import concourse.bacc as bacc
    from concourse.bass_utils import run_bass_kernel_spmd

    nc = bacc.Bacc("TRN2", target_bir_lowering=False, num_devices=1)
    arrays, args = {}, []
    for name in INS:
        a = np.ascontiguousarray(inputs[name])
        arrays[f"in_{name}"] = a
        args.append(nc.dram_tensor(f"in_{name}", a.shape, mybir.dt.from_np(a.dtype), kind="ExternalInput").ap())
    args.append(nc.dram_tensor("out_0", (B, M, D), mybir.dt.float32, kind="ExternalOutput").ap())
    build(nc, *args)
    r = run_bass_kernel_spmd(nc, [arrays], core_ids=[0])
    return r.results[0]["out_0"]
```

```python
from contextlib import ExitStack

import numpy as np
import concourse.bass as bass
from concourse import mybir

P = 128
B, M, D = 2, 1024, 2048
CTX = 2048
E, R = 8, 16
ER = E * R
TB = M // P
T = B * TB
KC = D // P
NW = 512
NB = D // NW
SLOTS = 6
PIECES = 4
PK = KC // PIECES
XS = 4
WC = ER + E
GK = KC // 4
EPS = 1e-5
QMAX = 255.0
ZC = 128.0
ROUND = 12582912.0
YS = 1024.0
WS = 32768.0
TINY = 1e-30


class Count:

    def __init__(self, reg, step, start):
        self.reg, self.step, self.start = reg, step, start

    def __add__(self, n):
        return Count(self.reg, self.step, self.start + n)

    def __sub__(self, n):
        return self + -n

    def __mul__(self, n):
        return Count(self.reg, self.step * n, self.start * n)

    __radd__, __rmul__ = __add__, __mul__

    def value(self):
        return self.reg * self.step + self.start


def at(n):
    return n if isinstance(n, int) else n.value()


def due(n):
    return not isinstance(n, int) or n > 0


def half(n):
    return n // 2 if isinstance(n, int) else Count(n.reg, n.step // 2, n.start // 2)


def build(nc, x, ctx, g_x, g_f, x1_scale, x1_zp, x2_scale, x2_zp, route_w, A, Bw, out):
    f32, bf16, f16 = mybir.dt.float32, mybir.dt.bfloat16, mybir.dt.float16
    i32, u32 = mybir.dt.int32, mybir.dt.uint32
    ALU = mybir.AluOpType
    ACT = mybir.ActivationFunctionType
    AX = mybir.AxisListType

    x_t = x.rearrange("b (t p) n -> (b t) p n", p=P)
    out_t = out.rearrange("b (t p) n -> (b t) p n", p=P)
    ctx_k = ctx.rearrange("b (c p) n -> b p c n", p=P)
    A_v = A.rearrange("e r d -> (e r) d")
    B_v = Bw.rearrange("e (p j) r -> p e j r", p=P)

    st = ExitStack()
    with st:
        def sb(name, shape, dt):
            return st.enter_context(nc.sbuf_tensor(name, shape, dt))

        def bank(name):
            return st.enter_context(nc.psum_tensor(name, [P, NW], f32))

        def sem(name):
            return st.enter_context(nc.semaphore(name))

        s_x_loaded = [sem("x_loaded0"), sem("x_loaded1")]
        s_early_loaded = [sem("early_loaded0"), sem("early_loaded1"), sem("early_loaded2"), sem("early_loaded3"),
                          sem("early_loaded4")]
        s_ctx_loaded = [sem("ctx_loaded0"), sem("ctx_loaded1"), sem("ctx_loaded2")]
        s_xw_loaded = sem("xw_loaded")
        s_par_loaded = sem("par_loaded")
        s_a_loaded = sem("a_loaded")
        s_r_loaded = sem("r_loaded")
        s_b_loaded = sem("b_loaded")
        s_stored = sem("stored")
        s_half_stored = sem("half_stored")
        s_id_zero = sem("id_zero")
        s_idf_made = sem("idf_made")
        s_consts = sem("consts")
        s_mexp_set = sem("mexp_set")
        s_eid_made = sem("eid_made")
        s_eid_ready = sem("eid_ready")
        s_inv_done = sem("inv_done")
        s_par_ready = sem("par_ready")
        s_dz_done = sem("dz_done")
        s_nz_done = sem("nz_done")
        s_flag_ready = sem("flag_ready")
        s_tanh_done = sem("tanh_done")
        s_s12_done = sem("s12_done")
        s_cc_done = sem("cc_done")
        s_cd_done = sem("cd_done")
        s_kdd_done = sem("kdd_done")
        s_wmax_step = sem("wmax_step")
        s_rmax_step = sem("rmax_step")
        s_bmax_step = sem("bmax_step")
        s_a_scale = sem("a_scale")
        s_r_scale = sem("r_scale")
        s_a_turned = sem("a_turned")
        s_r_turned = sem("r_turned")
        s_a_high = sem("a_high")
        s_r_high = sem("r_high")
        s_a_low = sem("a_low")
        s_r_low = sem("r_low")
        s_b_permuted = sem("b_permuted")
        s_b_turned = sem("b_turned")
        s_b_raw = sem("b_raw")
        s_b_high = sem("b_high")
        s_weights_ready = sem("weights_ready")
        s_wsc_step = sem("wsc_step")
        s_diag_ready = sem("diag_ready")
        s_scales_spread = sem("scales_spread")
        s_wscale_ready = sem("wscale_ready")
        s_ctx_affine = sem("ctx_affine")
        s_ctx_rounded = sem("ctx_rounded")
        s_ctx_ready = sem("ctx_ready")
        s_bn1_done = sem("bn1_done")
        s_stats1 = sem("stats1")
        s_ve1_done = sem("ve1_done")
        s_rs1_done = sem("rs1_done")
        s_na1_done = sem("na1_done")
        s_norm1 = sem("norm1")
        s_affine1 = sem("affine1")
        s_x_rounded = sem("x_rounded")
        s_q1_ready = sem("q1_ready")
        s_q1T_turned = sem("q1T_turned")
        s_q1T_ready = sem("q1T_ready")
        s_main_done = sem("main_done")
        s_main_added = sem("main_added")
        s_bn2_done = sem("bn2_done")
        s_stats2 = sem("stats2")
        s_ve2_done = sem("ve2_done")
        s_rs2_done = sem("rs2_done")
        s_na2_done = sem("na2_done")
        s_norm2 = sem("norm2")
        s_y_ready = sem("y_ready")
        s_y_turned = sem("y_turned")
        s_y_high = sem("y_high")
        s_y_split = sem("y_split")
        s_h_done = sem("h_done")
        s_hs_done = sem("hs_done")
        s_h_read = sem("h_read")
        s_hl_done = sem("hl_done")
        s_top_done = sem("top_done")
        s_idx_done = sem("idx_done")
        s_idxf_done = sem("idxf_done")
        s_pick_done = sem("pick_done")
        s_wh_done = sem("wh_done")
        s_am_done = sem("am_done")
        s_floor_done = sem("floor_done")
        s_rec_done = sem("rec_done")
        s_tsc_done = sem("tsc_done")
        s_wh_high = sem("wh_high")
        s_wh_ready = sem("wh_ready")
        s_wh_turned = sem("wh_turned")
        s_whT_ready = sem("whT_ready")
        s_out_done = sem("out_done")
        s_outp_read = sem("outp_read")
        s_colsum_done = sem("colsum_done")
        s_rowsum_done = sem("rowsum_done")
        s_rowc_ready = sem("rowc_ready")
        s_col_added = sem("col_added")
        s_terms_added = sem("terms_added")
        s_passed = sem("passed")

        q2 = sb("q2", [P, SLOTS, KC, NW], bf16)
        xs = sb("xs", [P, XS, D], f32)
        q1 = sb("q1", [P, D], bf16)
        q1T = sb("q1T", [P, 2, KC, P], bf16)
        xw = sb("xw", [P, D], f32)
        stage = sb("stage", [P, 3, PK * NW], f32)
        y = sb("y", [P, D], f32)
        yhi = sb("yhi", [P, 2, GK * P], f16)
        ylo = sb("ylo", [P, 2, GK * P], f16)
        WT = sb("WT", [P, KC, 2 * WC], f16)
        BT = sb("BT", [P, 2, D], f16)
        hs = sb("hs", [P, WC], f32)
        hl = sb("hl", [P, WC], f32)
        wscale = sb("wscale", [P, WC], f32)
        top8 = sb("top8", [P, 8], f32)
        idx8 = sb("idx8", [P, 8], u32)
        idxf = sb("idxf", [P, 1], f32)
        pick = sb("pick", [P, ER], f32)
        wh = sb("wh", [P, ER], f32)
        whs = sb("whs", [P, 2, ER], f16)
        whT = sb("whT", [P, 2, P], f16)
        am = sb("am", [P, 3], f32)
        tsc = sb("tsc", [P, 2], f32)
        eid_i = wh[:, :].bitcast(i32)
        eid = sb("eid", [P, ER], f32)
        idf = sb("idf", [P, P], f32)
        idb = sb("idb", [P, P], bf16)
        idh = sb("idh", [P, P], f16)
        onesf = sb("onesf", [P, P], f32)
        zero = sb("zero", [P, 1], f32)
        onesb = sb("onesb", [P, P], bf16)
        diag = pick
        diag8 = sb("diag8", [E, E], f32)
        par = sb("par", [P, 8], f32)
        inv = sb("inv", [P, 2], f32)
        ninv = sb("ninv", [P, 1], f32)
        th = sb("th", [P, 2], f32)
        c12 = sb("c12", [P, 2], f32)
        cc = sb("cc", [P, 1], f32)
        dz = sb("dz", [P, 2], f32)
        cd = sb("cd", [P, 2], f32)
        kdd = sb("kdd", [P, 2], f32)
        nz = sb("nz", [P, 2], f32)
        flag = sb("flag", [P, 1], f32)
        mexp = sb("mexp", [P, 1], f32)
        bn1 = sb("bn1", [P, NB, 6], f32)
        bn2 = sb("bn2", [P, NB, 6], f32)
        mv1 = sb("mv1", [P, 2, 2], f32)
        mv2 = sb("mv2", [P, 2, 2], f32)
        ve1 = sb("ve1", [P, 2], f32)
        ve2 = sb("ve2", [P, 2], f32)
        rs1 = sb("rs1", [P, 2], f32)
        rs2 = sb("rs2", [P, 2], f32)
        sc1 = sb("sc1", [P, 2, 3], f32)
        sc2 = sb("sc2", [P, 2, 3], f32)
        rowc = sb("rowc", [P, 2], f32)
        wmax = sb("wmax", [P, 3], f32)
        rmax = sb("rmax", [E, 3], f32)
        bmax = sb("bmax", [P, 3], f32)
        wsc = sb("wsc", [P, 2], f32)
        rsc = sb("rsc", [E, 1], f32)

        mainp = [bank("main0"), bank("main1")]
        turn = [bank("turn0"), bank("turn1")]
        turnb = [t[:, :].bitcast(bf16) for t in turn]
        hp = bank("hp")
        wp = bank("wp")
        wph = wp[:, :].bitcast(f16)
        outp = [bank("outp0"), bank("outp1")]

        scr = [q2[:, s, :, :].rearrange("p k n -> p (k n)").bitcast(f32) for s in (SLOTS - 2, SLOTS - 1)]
        a_nat, r_nat = scr[0][:, 0:D], scr[0][0:E, D:2 * D]
        b_nat, b_perm = scr[1][:, 0:D], scr[1][:, D:2 * D]
        b_raw = b_nat

        def xcol(t, c0, c1):
            if isinstance(t, int):
                return xs[:, t % XS, c0:c1]
            return xs[:, bass.ds(at(t) % XS, 1), c0:c1].rearrange("p a n -> p (a n)")

        def slot(block):
            return block % SLOTS

        EARLY = NB * PIECES
        LATE = EARLY + TB

        RING = 5
        XW = 3
        SWITCH = {LATE: (2, None), LATE + 1: (0, LATE - 2), LATE + 2: (1, LATE - 1), LATE + 3: (XW, None),
                  LATE + 4: (2, LATE), LATE + 5: (0, LATE + 1), LATE + 6: (1, LATE + 2), LATE + 7: (2, LATE + 4)}

        HELD_BY_POOL = range(LATE, LATE + 2)

        def in_q2(piece):
            block, q = piece // PIECES, piece % PIECES
            return q2[:, slot(block), q * PK:(q + 1) * PK, :].rearrange("p k n -> p (k n)")

        def place(piece, s=None):
            if s is not None:
                return stage[:, s, :]
            if piece < EARLY:
                return [xs[:, XS - 1, :], stage[:, 0, :], stage[:, 1, :], stage[:, 2, :], y[:, :]][piece % RING]
            if piece < LATE:
                return stage[:, piece % 2, :]
            return xw[:, :] if SWITCH[piece][0] == XW else stage[:, SWITCH[piece][0], :]

        def landed(piece):
            if piece < EARLY:
                return s_early_loaded[piece % RING], 16 * (piece // RING + 1)
            if piece < LATE:
                return s_ctx_loaded[piece % 2], 16 * ((piece - EARLY) // 2 + 1)
            here, before = SWITCH[piece]
            if here == XW:
                return s_xw_loaded, 16
            return s_ctx_loaded[here], 16 + (landed(before)[1] if before else 0)

        def schedule(eng, f, first=0):
            if first == 0:
                f(0, 0, True)
            f(1, 1, True)
            with eng.Fori(0, TB // 2 - 2) as pair:
                t = Count(pair, 2, 2)
                f(t, 0, True)
                f(t + 1, 1, True)
            for t in range(TB - 2, TB + 2):
                f(t, t % 2, t < TB)
            with eng.Fori(0, (T - TB) // 2 - 2) as pair:
                t = Count(pair, 2, TB + 2)
                f(t, 0, False)
                f(t + 1, 1, False)
            for t in range(T - 2, T + 2):
                f(t, t % 2, False)

        def has(t, d):
            return not isinstance(t, int) or 0 <= t + d < T

        block_ = st.enter_context(nc.Block())

        @block_.sync
        def _(sp):
            def load_x(t, pt):
                src = x_t[t] if isinstance(t, int) else x_t[bass.ds(at(t), 1)].rearrange("a p n -> p (a n)")
                sp.dma_start(xcol(t, 0, D), src).then_inc(s_x_loaded[pt], 16)

            def load_ctx(piece):
                b, nb, q = piece // (NB * PIECES), piece // PIECES % NB, piece % PIECES
                if piece < EARLY:
                    before = piece - RING
                elif piece < LATE:
                    before = piece - 2 if piece > EARLY + 1 else piece - RING
                else:
                    before = SWITCH[piece][1]
                if piece == LATE + 3:
                    sp.wait_ge(s_q1_ready, TB + 1)
                elif before is not None and before >= 0:
                    sp.wait_ge(s_ctx_rounded, before + 1)
                sp.dma_start(place(piece).rearrange("p (c n) -> p c n", c=PK),
                             ctx_k[b, :, q * PK:(q + 1) * PK, nb * NW:(nb + 1) * NW]).then_inc(landed(piece)[0], 16)

            load_x(0, 0)
            for n, v in enumerate((x1_scale, x2_scale, x1_zp, x2_zp, g_x, g_f)):
                sp.dma_start(par[:, n:n + 1], v.partition_broadcast(P)).then_inc(s_par_loaded, 16)
            for piece in range(EARLY):
                load_ctx(piece)
                if piece == 3:
                    sp.dma_start(a_nat, A_v).then_inc(s_a_loaded, 16)
                    sp.dma_start(r_nat, route_w).then_inc(s_r_loaded, 16)
                if piece == 10:
                    load_x(1, 1)
            load_ctx(EARLY)
            sp.dma_start(b_nat.rearrange("p (e j r) -> p e (j r)", e=E, r=R),
                         B_v.rearrange("p e j r -> p e (j r)")).then_inc(s_b_loaded, 16)
            load_ctx(EARLY + 1)
            load_x(2, 0)

            def loop_ctx(t, pt):
                n = t + 1
                sp.wait_ge(s_ctx_rounded, at(EARLY + n - 1))
                src = ctx_k[1, :, bass.ds(at(n) % PIECES * PK, PK), bass.ds(at(n) // PIECES * NW, NW)]
                sp.dma_start(stage[:, 1 - pt, :].rearrange("p (c n) -> p c n", c=PK), src)\
                  .then_inc(s_ctx_loaded[1 - pt], 16)

            def period(t, pt, batch0):
                ahead, between, behind = [], [], []
                if isinstance(t, int):
                    if 0 < t < TB - 1:
                        ahead = [EARLY + t + 1]
                    if t == TB - 2:
                        behind = [LATE, LATE + 1]
                    if t == TB - 1:
                        ahead, between, behind = [LATE + 2], [LATE + 3], [LATE + 4, LATE + 5]
                    if t == TB:
                        ahead = [LATE + 6, LATE + 7]
                elif batch0:
                    loop_ctx(t, pt)
                for piece in ahead:
                    load_ctx(piece)
                if isinstance(t, int) and t == T + 1:
                    sp.wait_ge(s_outp_read, 2 + NB * T - NB // 2)
                    sp.dma_start(out_t[T - 1][:, 0:D // 2], xcol(T - 1, 0, D // 2)).then_inc(s_stored, 16)
                    sp.wait_ge(s_outp_read, 2 + NB * T)
                    sp.dma_start(out_t[T - 1][:, D // 2:D], xcol(T - 1, D // 2, D)).then_inc(s_half_stored, 16)
                elif has(t, -2):
                    sp.wait_ge(s_outp_read, at(2 + NB * (t - 1)))
                    dst = out_t[t - 2] if isinstance(t, int) else out_t[bass.ds(at(t - 2), 1)]\
                        .rearrange("a p n -> p (a n)")
                    sp.dma_start(dst, xcol(t - 2, 0, D)).then_inc(s_stored, 16)
                for piece in between:
                    load_ctx(piece)
                if has(t, 2) and not (isinstance(t, int) and t == 0):
                    if isinstance(t, int) and t == 1:
                        sp.wait_ge(s_ctx_rounded, EARLY)
                    if due(16 * (t - 1)):
                        sp.wait_ge(s_stored, at(16 * (t - 1)))
                    load_x(t + 2, pt)
                for piece in behind:
                    load_ctx(piece)

            schedule(sp, period)
            sp.wait_ge(s_stored, 16 * T)
            sp.wait_ge(s_half_stored, 16)

        @block_.gpsimd
        def _(pool):
            pool.memset(idf[:, :], 0.0).then_inc(s_id_zero, 1)
            pool.sem_inc(s_outp_read, 2)
            pool.memset(onesf[:, :], 1.0).then_inc(s_consts, 1)
            pool.memset(onesb[:, :], 1.0).then_inc(s_consts, 1)
            pool.memset(zero[:, :], 0.0).then_inc(s_consts, 1)
            pool.memset(mexp[:, :], -0.5).then_inc(s_mexp_set, 1)
            pool.iota(eid_i, pattern=[[1, E], [0, R]], base=0, channel_multiplier=0).then_inc(s_eid_made, 1)
            pool.wait_ge(s_id_zero, 1)
            pool.affine_select(out=idf[:, :], in_=idf[:, :], compare_op=ALU.not_equal, fill=1.0, base=0,
                               pattern=[[-1, P]], channel_multiplier=1).then_inc(s_idf_made, 1)
            pool.wait_ge(s_idf_made, 1)
            pool.tensor_copy(idb[:, :], idf[:, :]).then_inc(s_consts, 1)
            pool.tensor_copy(idh[:, :], idf[:, :]).then_inc(s_consts, 1)
            pool.wait_ge(s_eid_made, 1)
            pool.tensor_copy(eid[:, :], eid_i).then_inc(s_eid_ready, 1)

            def first_norm(t, pt):
                pool.wait_ge(s_stats1, at(t + 1))
                pool.sem_inc(s_passed, 1)
                if isinstance(t, int) and t == 0:
                    pool.wait_ge(s_par_ready, 1)
                    pool.wait_ge(s_mexp_set, 1)
                if due(t - 1):
                    pool.wait_ge(s_affine1, at(t - 1))
                pool.sem_inc(s_passed, 1)
                pool.tensor_scalar(ve1[:, pt:pt + 1], mv1[:, pt, 1:2], EPS, None, ALU.add).then_inc(s_ve1_done, 1)
                pool.wait_ge(s_ve1_done, at(t + 1))
                pool.tensor_tensor(rs1[:, pt:pt + 1], ve1[:, pt:pt + 1], mexp[:, :], ALU.pow).then_inc(s_rs1_done, 1)
                pool.wait_ge(s_rs1_done, at(t + 1))
                pool.tensor_tensor(sc1[:, pt, 0:1], rs1[:, pt:pt + 1], ninv[:, :], ALU.mult).then_inc(s_na1_done, 1)
                pool.tensor_tensor(sc1[:, pt, 1:2], rs1[:, pt:pt + 1], inv[:, 0:1], ALU.mult)
                pool.wait_ge(s_na1_done, at(t + 1))
                pool.sem_inc(s_passed, 1)
                pool.tensor_scalar(sc1[:, pt, 2:3], mv1[:, pt, 0:1], sc1[:, pt, 0:1], par[:, 2:3], ALU.mult, ALU.add)\
                    .then_inc(s_norm1, 1)

            def second_norm(t, pt):
                pool.wait_ge(s_stats2, at(t + 1))
                if due(t - 1):
                    pool.wait_ge(s_y_ready, at(t - 1))
                pool.sem_inc(s_passed, 1)
                pool.tensor_scalar(ve2[:, pt:pt + 1], mv2[:, pt, 1:2], EPS, None, ALU.add).then_inc(s_ve2_done, 1)
                pool.wait_ge(s_ve2_done, at(t + 1))
                pool.tensor_tensor(rs2[:, pt:pt + 1], ve2[:, pt:pt + 1], mexp[:, :], ALU.pow).then_inc(s_rs2_done, 1)
                pool.wait_ge(s_rs2_done, at(t + 1))
                pool.sem_inc(s_passed, 1)
                pool.tensor_scalar(sc2[:, pt, 0:1], rs2[:, pt:pt + 1], -YS, None, ALU.mult).then_inc(s_na2_done, 1)
                pool.tensor_scalar(sc2[:, pt, 1:2], rs2[:, pt:pt + 1], YS, None, ALU.mult)
                pool.wait_ge(s_na2_done, at(t + 1))
                pool.tensor_tensor(sc2[:, pt, 2:3], mv2[:, pt, 0:1], sc2[:, pt, 0:1], ALU.mult).then_inc(s_norm2, 1)

            def hold_ctx(piece):
                pool.wait_ge(s_ctx_rounded, piece + 1)
                pool.tensor_scalar(in_q2(piece), in_q2(piece), -ZC, QMAX - ZC, ALU.max, ALU.min)\
                    .then_inc(s_ctx_ready, 1)

            first_norm(0, 0)

            def period(t, pt, batch0):
                last0, at_switch = isinstance(t, int) and t == TB - 1, isinstance(t, int) and t == TB
                if has(t, 1):
                    first_norm(t + 1, 1 - pt)
                if last0:
                    hold_ctx(LATE)
                    hold_ctx(LATE + 1)
                if has(t, 0):
                    second_norm(t, pt)

            schedule(pool, period)

        @block_.scalar
        def _(act):
            act.wait_ge(s_par_loaded, 16 * 6)
            act.activation(th[:, :], par[:, 4:6], ACT.Tanh).then_inc(s_tanh_done, 1)

            def affine_ctx(piece, n=None):
                if n is None:
                    act.wait_ge(landed(piece)[0], landed(piece)[1])
                else:
                    act.wait_ge(s_ctx_loaded[n], at(16 * (half(piece - EARLY) + 1)))
                act.activation(place(piece, n), place(piece, n), ACT.Identity, bias=par[:, 3:4], scale=inv[:, 1:2])\
                   .then_inc(s_ctx_affine, 1)

            def affine_x(t, pt):
                act.wait_ge(s_norm1, at(t + 1))
                if due(t):
                    act.wait_ge(s_q1_ready, at(t))
                if isinstance(t, int) and t == TB + 1:
                    act.wait_ge(s_ctx_rounded, LATE + 4)
                act.activation(xw[:, :], xcol(t, 0, D), ACT.Relu, bias=sc1[:, pt, 2:3], scale=sc1[:, pt, 1:2])\
                   .then_inc(s_affine1, 1)

            def finish_q1(t):
                act.wait_ge(s_x_rounded, at(t + 1))
                if due(2 * t):
                    act.wait_ge(s_q1T_turned, at(2 * t))
                act.activation(q1[:, :], xw[:, :], ACT.Copy, bias=-(ROUND + ZC)).then_inc(s_q1_ready, 1)

            def take_q1T(t, pt):
                for half in range(2):
                    act.wait_ge(s_q1T_turned, at(2 * t + half + 1))
                    act.activation(q1T[:, pt, half * KC // 2:(half + 1) * KC // 2, :].rearrange("p k m -> p (k m)"),
                                   turnb[half], ACT.Copy).then_inc(s_q1T_ready, 1)

            def a_high(c):
                act.wait_ge(s_a_turned, at(c + 1))
                act.activation(WT[:, GK * c:GK * (c + 1), 0:ER], turn[c % 2][:, :].rearrange("p (k m) -> p k m", k=GK),
                               ACT.Copy).then_inc(s_a_high, 1)

            def take_b(c):
                act.wait_ge(s_b_turned, c + 1)
                act.activation(b_raw.rearrange("e (p j) -> e j p", j=KC)[:, 4 * c:4 * c + 4, :],
                               turn[c % 2][:, :].rearrange("e (j p) -> e j p", j=4), ACT.Copy).then_inc(s_b_raw, 1)

            act.wait_ge(s_par_ready, 1)
            affine_ctx(0)
            affine_x(0, 0)
            affine_ctx(1)
            affine_ctx(2)
            affine_ctx(3)
            take_q1T(0, 0)
            affine_ctx(4)
            affine_ctx(5)
            affine_ctx(6)
            a_high(0)
            a_high(1)
            affine_ctx(7)
            a_high(2)
            a_high(3)
            affine_ctx(8)
            affine_ctx(9)
            affine_ctx(10)
            affine_ctx(11)
            act.wait_ge(s_r_turned, 1)
            act.activation(WT[:, :, ER:WC], wp[:, 0:KC * E].rearrange("p (k m) -> p k m", k=KC),
                           ACT.Copy).then_inc(s_r_high, 1)
            affine_ctx(12)
            affine_ctx(13)
            affine_x(1, 1)
            affine_ctx(14)
            affine_ctx(15)
            finish_q1(1)
            affine_ctx(EARLY)
            act.wait_ge(s_b_loaded, 16)
            act.activation(b_perm.rearrange("p (j e r) -> p e j r", e=E, r=R),
                           b_nat.rearrange("p (e j r) -> p e j r", e=E, r=R), ACT.Copy).then_inc(s_b_permuted, 1)
            affine_ctx(EARLY + 1)
            take_q1T(1, 1)

            def norm_group(g):
                c0, c1 = g * GK * P, (g + 1) * GK * P
                act.activation(y[:, c0:c1], xcol(T - 1, c0, c1), ACT.Identity, bias=sc2[:, 1, 2:3],
                               scale=sc2[:, 1, 1:2]).then_inc(s_y_ready, 1)

            def high_part(t, g):
                act.wait_ge(s_y_turned, at(4 * t + g + 1))
                act.activation(yhi[:, g % 2, :], turn[g % 2][:, :], ACT.Copy).then_inc(s_y_high, 1)

            def period(t, pt, batch0):
                last0, at_switch = isinstance(t, int) and t == TB - 1, isinstance(t, int) and t == TB
                last = isinstance(t, int) and t == T
                if has(t, -2):
                    if due(t - 1):
                        act.wait_ge(s_wh_turned, at(t - 1))
                    act.activation(whT[:, :, :].rearrange("p a m -> p (a m)"), wph[:, 0:2 * P], ACT.Copy)\
                       .then_inc(s_whT_ready, 1)
                if isinstance(t, int):
                    if t == 1:
                        for c in range(4):
                            take_b(c)
                    elif t < TB - 1:
                        affine_ctx(EARLY + t)
                    if last0:
                        affine_ctx(LATE)
                elif batch0:
                    affine_ctx(EARLY + t, pt)
                if has(t, -1):
                    if due(t):
                        act.wait_ge(s_norm2, at(t))
                    if due(4 * (t - 1)):
                        act.wait_ge(s_y_turned, at(4 * (t - 1)))
                    if last:
                        norm_group(0)
                        norm_group(1)
                    else:
                        act.activation(y[:, :], xcol(t - 1, 0, D), ACT.Identity, bias=sc2[:, 1 - pt, 2:3],
                                       scale=sc2[:, 1 - pt, 1:2]).then_inc(s_y_ready, 1)
                if at_switch:
                    affine_ctx(LATE + 4)
                if has(t, -1):
                    high_part(t - 1, 0)
                if at_switch:
                    affine_ctx(LATE + 5)
                if last:
                    norm_group(2)
                    norm_group(3)
                if has(t, 1):
                    affine_x(t + 1, 1 - pt)
                if has(t, -1):
                    high_part(t - 1, 1)
                if last0:
                    affine_ctx(LATE + 1)
                if at_switch:
                    affine_ctx(LATE + 6)
                if has(t, 1):
                    finish_q1(t + 1)
                if has(t, -1):
                    high_part(t - 1, 2)
                if has(t, -1):
                    high_part(t - 1, 3)
                if isinstance(t, int):
                    if t == 1:
                        act.wait_ge(s_consts, 5)
                        act.wait_ge(s_bmax_step, 3)
                        act.activation(BT[:, 0, :], b_raw, ACT.Identity, bias=zero[:, :], scale=bmax[:, 2:3])\
                           .then_inc(s_b_high, 1)
                    if last0:
                        affine_ctx(LATE + 2)
                    if at_switch:
                        affine_ctx(LATE + 7)
                if has(t, -1):
                    act.wait_ge(s_h_done, at(t))
                    act.activation(hs[:, :], hp[:, WC:2 * WC], ACT.Copy).then_inc(s_hs_done, 1)
                if has(t, 1):
                    take_q1T(t + 1, 1 - pt)
                if isinstance(t, int) and t == 1:
                    act.wait_ge(s_weights_ready, 1)
                if isinstance(t, int) and t == TB - 2:
                    affine_ctx(LATE - 1)
                if last0:
                    affine_ctx(LATE + 3)

            schedule(act, period, first=1)

        @block_.vector
        def _(dve):
            dve.wait_ge(s_par_loaded, 16 * 6)
            dve.reciprocal(inv[:, :], par[:, 0:2]).then_inc(s_inv_done, 1)
            dve.wait_ge(s_inv_done, 1)
            dve.tensor_scalar(ninv[:, :], inv[:, 0:1], -1.0, None, ALU.mult).then_inc(s_par_ready, 1)
            dve.tensor_scalar(dz[:, :], par[:, 2:4], -1.0, ZC, ALU.mult, ALU.add).then_inc(s_dz_done, 1)
            dve.tensor_scalar(nz[:, :], par[:, 2:4], ZC, None, ALU.not_equal).then_inc(s_nz_done, 1)
            dve.wait_ge(s_nz_done, 1)
            dve.tensor_tensor(flag[:, :], nz[:, 0:1], nz[:, 1:2], ALU.add).then_inc(s_flag_ready, 1)
            dve.wait_ge(s_tanh_done, 1)
            dve.tensor_tensor(c12[:, 0:1], par[:, 0:1], par[:, 1:2], ALU.mult).then_inc(s_s12_done, 1)
            dve.wait_ge(s_s12_done, 1)
            dve.tensor_tensor(cc[:, :], c12[:, 0:1], th[:, 0:1], ALU.mult).then_inc(s_cc_done, 1)
            dve.wait_ge(s_cc_done, 1)
            dve.wait_ge(s_dz_done, 1)
            dve.tensor_scalar(cd[:, :], dz[:, :], cc[:, :], None, ALU.mult).then_inc(s_cd_done, 1)
            dve.wait_ge(s_cd_done, 1)
            dve.tensor_scalar(kdd[:, 0:1], cd[:, 0:1], dz[:, 1:2], float(CTX), ALU.mult, ALU.mult)\
               .then_inc(s_kdd_done, 1)
            dve.wait_ge(s_kdd_done, 1)
            dve.wait_ge(s_flag_ready, 1)
            other_zp = dve.value_load(flag[0:1, 0:1].bitcast(i32))

            def stats1(t, pt):
                dve.wait_ge(s_x_loaded[pt], at(16 * (half(t) + 1)))
                dve.sem_inc(s_passed, 1)
                for nb in range(NB):
                    dve.bn_stats(bn1[:, nb, :], xcol(t, nb * NW, (nb + 1) * NW)).then_inc(s_bn1_done, 1)
                dve.wait_ge(s_bn1_done, at(NB * (t + 1)))
                if due(t - 1):
                    dve.wait_ge(s_norm1, at(t - 1))
                dve.sem_inc(s_passed, 1)
                dve.bn_aggr(mv1[:, pt, :], bn1[:, :, :].rearrange("p a b -> p (a b)")).then_inc(s_stats1, 1)

            def round_x(t):
                dve.wait_ge(s_affine1, at(t + 1))
                dve.tensor_scalar(xw[:, :], xw[:, :], QMAX, ROUND, ALU.min, ALU.add).then_inc(s_x_rounded, 1)

            def round_ctx(piece, s=None, dst=None):
                if dst is None:
                    block = piece // PIECES
                    dst = in_q2(piece)
                    if block >= SLOTS:
                        dve.wait_ge(s_main_done, NB * (TB - 1) + slot(block) + 1)
                    elif block == SLOTS - 2:
                        dve.wait_ge(s_a_low, 4)
                        dve.wait_ge(s_r_low, 1)
                dve.wait_ge(s_ctx_affine, at(piece + 1))
                dve.tensor_scalar(dst, place(piece, s), ROUND, ROUND + ZC, ALU.add, ALU.subtract)\
                   .then_inc(s_ctx_rounded, 1)
                if piece in HELD_BY_POOL:
                    return
                dve.wait_ge(s_ctx_rounded, at(piece + 1))
                if piece == HELD_BY_POOL[-1] + 1:
                    dve.wait_ge(s_ctx_ready, piece)
                dve.tensor_scalar(dst, dst, -ZC, QMAX - ZC, ALU.max, ALU.min).then_inc(s_ctx_ready, 1)

            def scale_of(dst, src, step):
                dve.tensor_reduce(dst[:, 0:1], src, AX.X, ALU.max, apply_absolute_value=True).then_inc(step, 1)
                dve.wait_ge(step, 1)
                dve.tensor_scalar(dst[:, 1:2], dst[:, 0:1], 1.0 / WS, TINY, ALU.mult, ALU.max).then_inc(step, 1)
                dve.wait_ge(step, 2)
                dve.reciprocal(dst[:, 2:3], dst[:, 1:2]).then_inc(step, 1)
                dve.wait_ge(step, 3)

            def a_low(c):
                dve.wait_ge(s_a_high, at(c + 1))
                dve.tensor_tensor(WT[:, GK * c:GK * (c + 1), WC:WC + ER],
                                  turn[c % 2][:, :].rearrange("p (k m) -> p k m", k=GK),
                                  WT[:, GK * c:GK * (c + 1), 0:ER], ALU.subtract).then_inc(s_a_low, 1)

            def spread_scales():
                dve.tensor_scalar(wsc[:, 0:1], wmax[:, 1:2], 1.0 / YS, None, ALU.mult).then_inc(s_wsc_step, 1)
                dve.wait_ge(s_wsc_step, 1)
                dve.tensor_scalar(wsc[:, 1:2], bmax[:, 1:2], wsc[:, 0:1], None, ALU.mult).then_inc(s_wsc_step, 1)
                dve.tensor_scalar(rsc[:, :], rmax[:, 1:2], 1.0 / YS, None, ALU.mult).then_inc(s_wsc_step, 1)
                dve.wait_ge(s_wsc_step, 3)
                dve.tensor_scalar(diag[:, :], idf[:, :], wsc[:, 1:2], None, ALU.mult).then_inc(s_diag_ready, 1)
                dve.tensor_scalar(diag8[:, :], idf[0:E, 0:E], rsc[:, :], None, ALU.mult).then_inc(s_diag_ready, 1)

            def finish_weights():
                dve.wait_ge(s_b_high, 1)
                dve.scalar_tensor_tensor(out=BT[:, 1, :], in0=b_raw, scalar=bmax[:, 2:3], in1=BT[:, 0, :],
                                         op0=ALU.mult, op1=ALU.subtract).then_inc(s_weights_ready, 1)

            def zero_point_terms(t, blocks):
                with dve.If(other_zp != 0):
                    if blocks[0] == 0:
                        dve.wait_ge(s_q1_ready, at(t + 1))
                        dve.tensor_reduce(rowc[:, 0:1], q1[:, :], AX.X, ALU.add).then_inc(s_rowsum_done, 1)
                        dve.wait_ge(s_rowsum_done, at(t + 1))
                        dve.tensor_scalar(rowc[:, 1:2], rowc[:, 0:1], cd[:, 1:2], kdd[:, 0:1], ALU.mult, ALU.add)\
                           .then_inc(s_rowc_ready, 1)
                        dve.wait_ge(s_rowc_ready, at(t + 1))
                    for nb in blocks:
                        x_nb = xcol(t, nb * NW, (nb + 1) * NW)
                        dve.wait_ge(s_colsum_done, at(NB * t + nb + 1))
                        dve.scalar_tensor_tensor(out=x_nb, in0=wp[:, :], scalar=cd[:, 0:1], in1=x_nb,
                                                 op0=ALU.mult, op1=ALU.add).then_inc(s_col_added, 1)
                        dve.wait_ge(s_col_added, at(NB * t + nb + 1))
                        dve.tensor_scalar(x_nb, x_nb, rowc[:, 1:2], None, ALU.add).then_inc(s_terms_added, 1)
                        dve.wait_ge(s_terms_added, at(NB * t + nb + 1))
                    dve.sem_inc(s_passed, 1)
                    dve.nop()

            def add_main(t, pt, nb):
                c0, c1 = nb * NW, (nb + 1) * NW
                dve.wait_ge(s_main_done, at(NB * t + nb + 1))
                dve.scalar_tensor_tensor(out=xcol(t, c0, c1), in0=mainp[nb % 2][:, :], scalar=cc[:, :],
                                         in1=xcol(t, c0, c1), op0=ALU.mult, op1=ALU.add).then_inc(s_main_added, 1)

            def stats2(t, nb):
                dve.wait_ge(s_main_added, at(NB * t + nb + 1))
                dve.sem_inc(s_passed, 1)
                c0, c1 = nb * NW, (nb + 1) * NW
                dve.bn_stats(bn2[:, nb, :], xcol(t, c0, c1)).then_inc(s_bn2_done, 1)

            def gate(t, pt):
                n = t + 1
                dve.wait_ge(s_hs_done, at(n))
                dve.tensor_tensor(hl[:, :], hp[:, 0:WC], hs[:, :], ALU.add).then_inc(s_h_read, 1)
                dve.wait_ge(s_h_read, at(n))
                dve.tensor_tensor(hl[:, :], hl[:, :], wscale[:, :], ALU.mult).then_inc(s_hl_done, 1)
                dve.wait_ge(s_hl_done, at(n))
                dve.sem_inc(s_passed, 1)
                dve.max(top8[:, :], hl[:, ER:WC]).then_inc(s_top_done, 1)
                dve.wait_ge(s_top_done, at(n))
                dve.sem_inc(s_passed, 1)
                dve.max_index(idx8[:, :], top8[:, :], hl[:, ER:WC]).then_inc(s_idx_done, 1)
                dve.wait_ge(s_idx_done, at(n))
                dve.tensor_copy(idxf[:, :], idx8[:, 0:1]).then_inc(s_idxf_done, 1)
                dve.wait_ge(s_idxf_done, at(n))
                dve.tensor_scalar(pick[:, :], eid[:, :], idxf[:, :], top8[:, 0:1], ALU.is_equal, ALU.mult)\
                   .then_inc(s_pick_done, 1)
                dve.wait_ge(s_pick_done, at(n))
                dve.tensor_tensor(wh[:, :], hl[:, 0:ER], pick[:, :], ALU.mult).then_inc(s_wh_done, 1)
                dve.wait_ge(s_wh_done, at(n))
                dve.tensor_reduce(am[:, 0:1], wh[:, :], AX.X, ALU.max, apply_absolute_value=True).then_inc(s_am_done, 1)
                dve.wait_ge(s_am_done, at(n))
                dve.tensor_scalar(am[:, 1:2], am[:, 0:1], 1.0 / WS, TINY, ALU.mult, ALU.max).then_inc(s_floor_done, 1)
                dve.wait_ge(s_floor_done, at(n))
                dve.reciprocal(am[:, 2:3], am[:, 1:2]).then_inc(s_rec_done, 1)
                dve.tensor_scalar(tsc[:, pt:pt + 1], am[:, 1:2], th[:, 1:2], None, ALU.mult).then_inc(s_tsc_done, 1)
                dve.wait_ge(s_rec_done, at(n))
                dve.tensor_scalar(whs[:, 0, :], wh[:, :], am[:, 2:3], None, ALU.mult).then_inc(s_wh_high, 1)
                dve.wait_ge(s_wh_high, at(n))
                dve.scalar_tensor_tensor(out=whs[:, 1, :], in0=wh[:, :], scalar=am[:, 2:3], in1=whs[:, 0, :],
                                         op0=ALU.mult, op1=ALU.subtract).then_inc(s_wh_ready, 1)
                dve.wait_ge(s_tsc_done, at(n))
                dve.sem_inc(s_passed, 1)

            def stats2_sum(t, pt):
                dve.wait_ge(s_bn2_done, at(NB * (t + 1)))
                if due(t - 1):
                    dve.wait_ge(s_norm2, at(t - 1))
                dve.sem_inc(s_passed, 1)
                dve.bn_aggr(mv2[:, pt, :], bn2[:, :, :].rearrange("p a b -> p (a b)")).then_inc(s_stats2, 1)

            def add_experts(t, pt, g):
                dve.wait_ge(s_out_done, at(NB * t + g + 1))
                dve.scalar_tensor_tensor(out=xcol(t, g * NW, (g + 1) * NW), in0=outp[g % 2][:, :],
                                         scalar=tsc[:, pt:pt + 1], in1=xcol(t, g * NW, (g + 1) * NW),
                                         op0=ALU.mult, op1=ALU.add).then_inc(s_outp_read, 1)

            def low_part(t, g):
                dve.wait_ge(s_y_high, at(4 * t + g + 1))
                dve.tensor_tensor(ylo[:, g % 2, :], turn[g % 2][:, :], yhi[:, g % 2, :], ALU.subtract)\
                   .then_inc(s_y_split, 1)

            def period(t, pt, batch0):
                first = isinstance(t, int) and t % TB == 0 and t < T
                last0 = isinstance(t, int) and t == TB - 1
                at_switch = isinstance(t, int) and t == TB
                here, before, experts, after = has(t, 0), has(t, -1), has(t, -2), has(t, 1)
                if here:
                    zero_point_terms(t, (0,) if first else range(NB))
                if last0:
                    round_ctx(LATE - 1)
                if at_switch:
                    round_ctx(LATE + 3)
                    add_experts(t - 2, pt, 0)
                if after:
                    stats1(t + 1, 1 - pt)
                if experts and not at_switch:
                    add_experts(t - 2, pt, 0)
                if here:
                    add_main(t, pt, 0)
                if experts:
                    add_experts(t - 2, pt, 1)
                if at_switch:
                    round_ctx(LATE + 4)
                if first:
                    zero_point_terms(t, (1,))
                if isinstance(t, int) and t == 1:
                    dve.wait_ge(s_b_raw, 4)
                    scale_of(bmax, b_raw, s_bmax_step)
                    spread_scales()
                if here and not at_switch:
                    stats2(t, 0)
                if last0:
                    round_ctx(LATE)
                if experts:
                    add_experts(t - 2, pt, 2)
                if before:
                    low_part(t - 1, 0)
                if after:
                    round_x(t + 1)
                if before:
                    low_part(t - 1, 1)
                if at_switch:
                    round_ctx(LATE + 5)
                if experts:
                    add_experts(t - 2, pt, 3)
                if here:
                    add_main(t, pt, 1)
                if first:
                    zero_point_terms(t, (2,))
                if last0:
                    round_ctx(LATE + 1)
                if before:
                    low_part(t - 1, 2)
                if here and not at_switch:
                    stats2(t, 1)
                if before:
                    low_part(t - 1, 3)
                if at_switch:
                    round_ctx(LATE + 6)
                if isinstance(t, int):
                    if t == 1:
                        finish_weights()
                    elif t < TB - 1:
                        round_ctx(EARLY + t)
                elif batch0:
                    dst = q2[:, bass.ds(at(t) // PIECES + NB, 1), bass.ds(at(t) % PIECES * PK, PK), :]\
                        .rearrange("p a k n -> p (a k n)")
                    round_ctx(EARLY + t, pt, dst)
                if here:
                    add_main(t, pt, 2)
                if at_switch:
                    round_ctx(LATE + 7)
                    stats2(t, 0)
                    stats2(t, 1)
                if first:
                    zero_point_terms(t, (3,))
                if here:
                    stats2(t, 2)
                if isinstance(t, int) and t == 1:
                    dve.wait_ge(s_scales_spread, 1)
                    dve.tensor_copy(wscale[:, :], outp[0][:, 0:WC]).then_inc(s_wscale_ready, 1)
                    dve.wait_ge(s_wscale_ready, 1)
                    dve.wait_ge(s_weights_ready, 1)
                    dve.sem_inc(s_passed, 1)
                if before:
                    gate(t - 1, 1 - pt)
                if here:
                    add_main(t, pt, 3)
                    stats2(t, 3)
                    stats2_sum(t, pt)
                if last0:
                    round_ctx(LATE + 2)

            stats1(0, 0)
            round_ctx(0)
            round_x(0)
            dve.wait_ge(s_x_rounded, 1)
            dve.tensor_scalar(q1[:, :], xw[:, :], ROUND + ZC, None, ALU.subtract).then_inc(s_q1_ready, 1)
            for piece in range(1, 4):
                round_ctx(piece)
            zero_point_terms(0, (0,))
            dve.wait_ge(s_a_loaded, 16)
            round_ctx(4)
            scale_of(wmax, a_nat, s_wmax_step)
            dve.wait_ge(s_idf_made, 1)
            dve.tensor_scalar(diag[:, :], idf[:, :], wmax[:, 2:3], None, ALU.mult).then_inc(s_a_scale, 1)
            round_ctx(5)
            dve.wait_ge(s_r_loaded, 16)
            scale_of(rmax, r_nat, s_rmax_step)
            dve.tensor_scalar(diag8[:, :], idf[0:E, 0:E], rmax[:, 2:3], None, ALU.mult).then_inc(s_r_scale, 1)
            round_ctx(6)
            add_main(0, 0, 0)
            a_low(0)
            a_low(1)
            round_ctx(7)
            stats2(0, 0)
            a_low(2)
            a_low(3)
            zero_point_terms(0, (1,))
            round_ctx(8)
            round_ctx(9)
            round_ctx(10)
            add_main(0, 0, 1)
            stats1(1, 1)
            round_ctx(11)
            dve.wait_ge(s_r_high, 1)
            dve.tensor_tensor(WT[:, :, WC + ER:2 * WC], wp[:, 0:KC * E].rearrange("p (k m) -> p k m", k=KC),
                              WT[:, :, ER:WC], ALU.subtract).then_inc(s_r_low, 1)
            zero_point_terms(0, (2,))
            stats2(0, 1)
            round_ctx(12)
            round_ctx(13)
            round_ctx(14)
            round_x(1)
            round_ctx(15)
            add_main(0, 0, 2)
            zero_point_terms(0, (3,))
            stats2(0, 2)
            round_ctx(EARLY)
            round_ctx(EARLY + 1)
            dve.wait_ge(s_eid_ready, 1)
            add_main(0, 0, 3)
            stats2(0, 3)
            stats2_sum(0, 0)
            schedule(dve, period, first=1)

        @block_.tensor
        def _(pe):
            pe.wait_ge(s_flag_ready, 1)
            other_zp = pe.value_load(flag[0:1, 0:1].bitcast(i32))
            pe.wait_ge(s_idf_made, 1)
            pe.wait_ge(s_consts, 5)

            def turn_q1(t, half):
                for k in range(KC // 2):
                    c = half * KC // 2 + k
                    last = pe.transpose(turnb[half][:, k * P:(k + 1) * P], q1[:, c * P:(c + 1) * P], idb[:, :])
                last.then_inc(s_q1T_turned, 1)

            def turn_a():
                pe.wait_ge(s_a_scale, 1)
                for c in range(4):
                    if c < 2:
                        pe.wait_ge(s_q1T_ready, c + 1)
                    else:
                        pe.wait_ge(s_a_low, c - 1)
                    for k in range(GK):
                        last = pe.matmul(turn[c % 2][:, k * P:(k + 1) * P],
                                         a_nat[:, (GK * c + k) * P:(GK * c + k + 1) * P], diag[:, :],
                                         start=True, stop=True)
                    last.then_inc(s_a_turned, 1)

            def turn_router():
                pe.wait_ge(s_r_scale, 1)
                for k in range(KC):
                    last = pe.matmul(wp[:, k * E:(k + 1) * E], r_nat[:, k * P:(k + 1) * P], diag8[:, :],
                                     start=True, stop=True)
                last.then_inc(s_r_turned, 1)

            def turn_b(chunks):
                bj = b_perm.rearrange("p (j m) -> p j m", m=ER)
                for c in chunks:
                    if c == 0:
                        pe.wait_ge(s_b_permuted, 1)
                        pe.wait_ge(s_q1T_ready, 4)
                    if c >= 2:
                        pe.wait_ge(s_b_raw, c - 1)
                    for j in range(4):
                        last = pe.transpose(turn[c % 2][:, j * P:(j + 1) * P], bj[:, 4 * c + j], idf[:, :])
                    last.then_inc(s_b_turned, 1)

            def spread_scales():
                pe.wait_ge(s_diag_ready, 2)
                pe.matmul(outp[0][:, 0:ER], onesf[:, :], diag[:, :], start=True, stop=True)
                pe.matmul(outp[0][:, ER:WC], onesf[0:E, :], diag8[:, :], start=True, stop=True)\
                  .then_inc(s_scales_spread, 1)

            def column_sums(t, b, blocks):
                with pe.If(other_zp != 0):
                    for nb in blocks:
                        pe.wait_ge(s_ctx_ready, at(PIECES * (NB * b + nb + 1)))
                        if isinstance(t, int) and t == 0 and nb == 2:
                            pe.wait_ge(s_r_low, 1)
                        for k in range(KC):
                            last = pe.matmul(wp[:, :], onesb[:, :], q2[:, slot(NB * b + nb), k, :],
                                             start=(k == 0), stop=(k == KC - 1))
                        last.then_inc(s_colsum_done, 1)
                        pe.wait_ge(s_terms_added, at(NB * t + nb + 1))
                    pe.sem_inc(s_passed, 1)
                    pe.nop()

            def main(t, pt, b, nb, between):
                pe.wait_ge(s_ctx_ready, at(PIECES * (NB * b + nb + 1)))
                if due(NB * t + nb - 1):
                    pe.wait_ge(s_main_added, at(NB * t + nb - 1))
                for run in range(4):
                    for k in range(4 * run, 4 * run + 4):
                        last = pe.matmul(mainp[nb % 2][:, :], q1T[:, pt, k, :], q2[:, slot(NB * b + nb), k, :],
                                         start=(k == 0), stop=(k == KC - 1))
                    if run == 3:
                        last.then_inc(s_main_done, 1)
                    between(run)

            def expert_product(t, g):
                pe.wait_ge(s_outp_read, at(NB * t + g + 1))
                o = outp[g % 2][:, :]
                pe.matmul(o, whT[:, 0, :], BT[:, 0, g * NW:(g + 1) * NW], start=True, stop=False)
                pe.matmul(o, whT[:, 0, :], BT[:, 1, g * NW:(g + 1) * NW], start=False, stop=False)
                pe.matmul(o, whT[:, 1, :], BT[:, 0, g * NW:(g + 1) * NW], start=False, stop=True)\
                  .then_inc(s_out_done, 1)

            def turn_y(t, g):
                if g == 0:
                    pe.wait_ge(s_y_ready, at(t + 1))
                elif isinstance(t, int) and t == T - 1:
                    pe.wait_ge(s_y_ready, T + g)
                if g >= 2:
                    pe.wait_ge(s_y_split, at(4 * t + g - 1))
                for k in range(GK):
                    c = GK * g + k
                    last = pe.transpose(turn[g % 2][:, k * P:(k + 1) * P], y[:, c * P:(c + 1) * P], idf[:, :])
                last.then_inc(s_y_turned, 1)

            def h_product(t, g):
                if g == 0:
                    if due(t):
                        pe.wait_ge(s_h_read, at(t))
                pe.wait_ge(s_y_split, at(4 * t + g + 1))
                for k in range(GK):
                    c = GK * g + k
                    pe.matmul(hp[:, 0:2 * WC], yhi[:, g % 2, k * P:(k + 1) * P], WT[:, c, :],
                              start=(c == 0), stop=False, skip_group_check=True)
                    last = pe.matmul(hp[:, WC:2 * WC], ylo[:, g % 2, k * P:(k + 1) * P], WT[:, c, 0:WC],
                                     start=False, stop=(c == KC - 1), skip_group_check=True)
                if g == 3:
                    last.then_inc(s_h_done, 1)

            def period(t, pt, batch0):
                first = isinstance(t, int) and t % TB == 0 and t < T
                before, experts, after = has(t, -1), has(t, -2), has(t, 1)
                b = 0 if batch0 else 1

                def unit(nb, between):
                    if first:
                        column_sums(t, b, (nb,))
                    if has(t, 0):
                        main(t, pt, b, nb, between)
                    else:
                        for run in range(4):
                            between(run)

                def unit0(run):
                    if experts and run == 0:
                        if due(t - 1):
                            pe.wait_ge(s_wh_ready, at(t - 1))
                        for part in range(2):
                            last = pe.transpose(wph[:, part * P:(part + 1) * P], whs[:, part, :], idh[:, :])
                        last.then_inc(s_wh_turned, 1)
                    if experts and run == 1:
                        if due(t - 1):
                            pe.wait_ge(s_whT_ready, at(t - 1))
                        expert_product(t - 2, 0)
                    if experts and run == 3:
                        expert_product(t - 2, 1)
                    if isinstance(t, int) and t == 1 and run < 2:
                        turn_b((2 * run, 2 * run + 1))

                def unit1(run):
                    if isinstance(t, int) and t == 1:
                        if run in (1, 2):
                            pe.wait_ge(s_b_raw, run + 2)
                    if before and run == 1:
                        turn_y(t - 1, 0)
                    if experts and run == 1:
                        expert_product(t - 2, 2)
                    if before and run == 2:
                        turn_y(t - 1, 1)
                    if experts and run == 3:
                        expert_product(t - 2, 3)

                def unit2(run):
                    if before:
                        h_product(t - 1, run)
                        if run < 2:
                            turn_y(t - 1, run + 2)

                def unit3(run):
                    if after and run < 2:
                        if run == 0:
                            pe.wait_ge(s_q1_ready, at(t + 2))
                        if isinstance(t, int) and t == 0:
                            pe.wait_ge(s_a_low, run + 3)
                        if due(4 * (t - 1) + run + 3):
                            pe.wait_ge(s_y_split, at(4 * (t - 1) + run + 3))
                        turn_q1(t + 1, run)

                if has(t, 0) and not first:
                    column_sums(t, b, range(NB))
                if has(t, 0):
                    pe.wait_ge(s_q1T_ready, at(2 * (t + 1)))
                unit(0, unit0)
                if isinstance(t, int) and t == 0:
                    turn_a()
                unit(1, unit1)
                if isinstance(t, int) and t == 0:
                    turn_router()
                if isinstance(t, int) and t == 1:
                    spread_scales()
                unit(2, unit2)
                unit(3, unit3)

            pe.wait_ge(s_q1_ready, 1)
            turn_q1(0, 0)
            turn_q1(0, 1)
            schedule(pe, period)


INS = ['x', 'ctx_4096', 'g_xattn', 'g_ffn', 'L0_xattn_x1_scale', 'L0_xattn_x1_zp', 'L0_xattn_x2_scale',
       'L0_xattn_x2_zp', 'L0_ffn_route_w', 'L0_ffn_A', 'L0_ffn_Bw']


def kernel(**inputs):
    import concourse.bacc as bacc
    from concourse.bass_utils import run_bass_kernel_spmd

    nc = bacc.Bacc("TRN2", target_bir_lowering=False, num_devices=1)
    arrays, args = {}, []
    for name in INS:
        a = np.ascontiguousarray(inputs[name])
        arrays[f"in_{name}"] = a
        args.append(nc.dram_tensor(f"in_{name}", a.shape, mybir.dt.from_np(a.dtype), kind="ExternalInput").ap())
    args.append(nc.dram_tensor("out_0", (B, M, D), mybir.dt.float32, kind="ExternalOutput").ap())
    build(nc, *args)
    r = run_bass_kernel_spmd(nc, [arrays], core_ids=[0])
    return r.results[0]["out_0"]
```
